# Optimizing a Trainium2 kernel written in Bass

```python
import numpy as np
import jax
import jax.numpy as jnp

def _softmax(x, axis=-1):
    return jax.nn.softmax(x, axis=axis)

def _gelu(x):
    return jax.nn.gelu(x, approximate=True)

def _silu(x):
    return jax.nn.silu(x)

def _sigmoid(x):
    return jax.nn.sigmoid(x)

def _layernorm(x, axis=-1, eps=1e-05):
    m = jnp.mean(x, axis=axis, keepdims=True)
    v = jnp.var(x, axis=axis, keepdims=True)
    return (x - m) / jnp.sqrt(v + eps)

def _scatter_add(tgt, idx, src, axis=0):
    return tgt.at[idx].add(src)

def _segment_sum(src, seg, n):
    return jax.ops.segment_sum(src, seg, n)
kernel_name = 'mk_gnn_resnorm_d2_gnn_r8_822bdc'

def setup_inputs(seed: int=0):
    np.random.seed(seed)
    _w = jnp.asarray

    def _rec_inputs():
        import jax
        import jax.numpy as jnp
        _gk = jax.random.key(seed)
        x = -0.000202 + 1 * jax.random.normal(jax.random.fold_in(_gk, 1), (12500, 64), jnp.float32)
        src = jax.random.randint(jax.random.fold_in(_gk, 2), (200000,), 0, 12500, jnp.int32)
        dst = jnp.minimum((12500 * jax.random.uniform(jax.random.fold_in(_gk, 3), (200000,)) ** 2.0).astype(jnp.int32), 99999)
        _o = jnp.argsort(dst, stable=True)
        src = src[_o]
        dst = dst[_o]
        edge_attr_32 = -8.62073e-06 + 0.999901 * jax.random.normal(jax.random.fold_in(_gk, 12), (200000, 32), jnp.float32)
        edge_type_8 = jax.random.randint(jax.random.fold_in(_gk, 14), (200000,), 0, 8, jnp.int32)
        edge_weight1 = jax.random.uniform(jax.random.fold_in(_gk, 15), (200000, 1), jnp.float32, 0.0, 0.999998)
        return (x, src, dst, edge_attr_32, edge_type_8, edge_weight1)
    x, src, dst, edge_attr_32, edge_type_8, edge_weight1 = _rec_inputs()

    def _L0_gnn_setup():
        import jax, jax.numpy as jnp
        import numpy as np
        N_NODES = 12500
        N_EDGES = 125000
        NODE_DIM = 64
        EDGE_DIM = 32
        EPS = 1e-05
        SLOPE = 0.1

        def _mlp2(v, W1, b1, W2, b2):
            h = jax.nn.leaky_relu(v @ W1 + b1, negative_slope=SLOPE)
            return h @ W2 + b2
        key = jax.random.key(seed)
        ks = jax.random.split(key, 8)
        s = 0.05
        return {'x': jax.random.normal(ks[0], (N_NODES, NODE_DIM), dtype=jnp.float32), 'edge_attr': jax.random.normal(ks[1], (N_EDGES, EDGE_DIM), dtype=jnp.float32), 'W1n': jax.random.normal(ks[2], (NODE_DIM, 2 * NODE_DIM), dtype=jnp.float32) * s, 'b1n': jnp.zeros((2 * NODE_DIM,), dtype=jnp.float32), 'W2n': jax.random.normal(ks[3], (2 * NODE_DIM, NODE_DIM), dtype=jnp.float32) * s, 'b2n': jnp.zeros((NODE_DIM,), dtype=jnp.float32), 'W1e': jax.random.normal(ks[4], (EDGE_DIM, NODE_DIM), dtype=jnp.float32) * s, 'b1e': jnp.zeros((NODE_DIM,), dtype=jnp.float32), 'W2e': jax.random.normal(ks[5], (NODE_DIM, NODE_DIM), dtype=jnp.float32) * s, 'b2e': jnp.zeros((NODE_DIM,), dtype=jnp.float32), 'res_w': jnp.ones((1,), dtype=jnp.float32), 'dp_scale': jnp.ones((1,), dtype=jnp.float32), 'gamma': jnp.ones((NODE_DIM,), dtype=jnp.float32), 'beta': jnp.zeros((NODE_DIM,), dtype=jnp.float32), 'edge_index': jax.random.randint(ks[6], (2, N_EDGES), 0, N_NODES, dtype=jnp.int64) if jax.config.jax_enable_x64 else jax.random.randint(ks[6], (2, N_EDGES), 0, N_NODES, dtype=jnp.int32)}
    _L0_gnn_all = _L0_gnn_setup()
    _L0_gnn_in = {k: v for k, v in _L0_gnn_all.items() if k in ('W1n', 'b1n', 'W2n', 'b2n', 'W1e', 'b1e', 'W2e', 'b2e', 'res_w', 'dp_scale', 'gamma', 'beta')}
    del _L0_gnn_all

    def _L1_gnn_setup():
        import jax, jax.numpy as jnp
        import numpy as np
        N_NODES = 12500
        N_EDGES = 200000
        IN_FEAT = 64
        OUT_FEAT = 64
        NUM_RELS = 8
        NUM_BASES = 4
        key = jax.random.key(seed)
        ks = jax.random.split(key, 7)
        x = jax.random.normal(ks[0], (N_NODES, IN_FEAT), dtype=jnp.float32)
        src = jax.random.randint(ks[1], (N_EDGES,), 0, N_NODES, dtype=jnp.int32)
        dst = jax.random.randint(ks[2], (N_EDGES,), 0, N_NODES, dtype=jnp.int32)
        etypes = jax.random.randint(ks[3], (N_EDGES,), 0, NUM_RELS, dtype=jnp.int32)
        norm = jax.random.uniform(ks[4], (N_EDGES, 1), dtype=jnp.float32)
        limit_w = float(np.sqrt(2.0) * np.sqrt(6.0 / (IN_FEAT + OUT_FEAT)))
        weight = jax.random.uniform(ks[5], (NUM_BASES, IN_FEAT, OUT_FEAT), dtype=jnp.float32, minval=-limit_w, maxval=limit_w)
        limit_c = float(np.sqrt(2.0) * np.sqrt(6.0 / (NUM_RELS + NUM_BASES)))
        w_comp = jax.random.uniform(ks[6], (NUM_RELS, NUM_BASES), dtype=jnp.float32, minval=-limit_c, maxval=limit_c)
        h_bias = jnp.zeros((OUT_FEAT,), dtype=jnp.float32)
        return {'x': x, 'weight': weight, 'w_comp': w_comp, 'h_bias': h_bias, 'norm': norm, 'src': src, 'dst': dst, 'etypes': etypes}
    _L1_gnn_all = _L1_gnn_setup()
    _L1_gnn_in = {k: v for k, v in _L1_gnn_all.items() if k in ('weight', 'w_comp', 'h_bias')}
    del _L1_gnn_all
    return {'x': x, 'src': src, 'dst': dst, 'edge_attr_32': edge_attr_32, 'edge_type_8': edge_type_8, 'edge_weight1': edge_weight1, 'L0_gnn_W1n': _L0_gnn_in['W1n'], 'L0_gnn_b1n': _L0_gnn_in['b1n'], 'L0_gnn_W2n': _L0_gnn_in['W2n'], 'L0_gnn_b2n': _L0_gnn_in['b2n'], 'L0_gnn_W1e': _L0_gnn_in['W1e'], 'L0_gnn_b1e': _L0_gnn_in['b1e'], 'L0_gnn_W2e': _L0_gnn_in['W2e'], 'L0_gnn_b2e': _L0_gnn_in['b2e'], 'L0_gnn_res_w': _L0_gnn_in['res_w'], 'L0_gnn_dp_scale': _L0_gnn_in['dp_scale'], 'L0_gnn_gamma': _L0_gnn_in['gamma'], 'L0_gnn_beta': _L0_gnn_in['beta'], 'L1_gnn_weight': _L1_gnn_in['weight'], 'L1_gnn_w_comp': _L1_gnn_in['w_comp'], 'L1_gnn_h_bias': _L1_gnn_in['h_bias']}

def reference(x, src, dst, edge_attr_32, edge_type_8, edge_weight1, L0_gnn_W1n, L0_gnn_b1n, L0_gnn_W2n, L0_gnn_b2n, L0_gnn_W1e, L0_gnn_b1e, L0_gnn_W2e, L0_gnn_b2e, L0_gnn_res_w, L0_gnn_dp_scale, L0_gnn_gamma, L0_gnn_beta, L1_gnn_weight, L1_gnn_w_comp, L1_gnn_h_bias):
    import jax
    import jax.numpy as jnp

    def _L0_gnn_ref(x, edge_attr, W1n, b1n, W2n, b2n, W1e, b1e, W2e, b2e, res_w, dp_scale, gamma, beta, edge_index):
        import jax, jax.numpy as jnp
        import numpy as np
        N_NODES = 12500
        N_EDGES = 125000
        NODE_DIM = 64
        EDGE_DIM = 32
        EPS = 1e-05
        SLOPE = 0.1

        def _mlp2(v, W1, b1, W2, b2):
            h = jax.nn.leaky_relu(v @ W1 + b1, negative_slope=SLOPE)
            return h @ W2 + b2
        num_nodes = x.shape[0]
        x_t = _mlp2(x, W1n, b1n, W2n, b2n)
        e_t = _mlp2(edge_attr, W1e, b1e, W2e, b2e)
        src, dst = (edge_index[0], edge_index[1])
        msgs = x_t[src] * e_t * dp_scale
        aggregated = jax.ops.segment_sum(msgs, dst, num_segments=num_nodes)
        out = x + aggregated * res_w
        mu = jnp.mean(out, axis=-1, keepdims=True)
        var = jnp.mean(jnp.square(out - mu), axis=-1, keepdims=True)
        return (out - mu) * jax.lax.rsqrt(var + EPS) * gamma + beta

    def _L1_gnn_ref(x, weight, w_comp, h_bias, norm, src, dst, etypes):
        import jax, jax.numpy as jnp
        import numpy as np
        N_NODES = 12500
        N_EDGES = 200000
        IN_FEAT = 64
        OUT_FEAT = 64
        NUM_RELS = 8
        NUM_BASES = 4
        rel_w = jnp.einsum('rb,bio->rio', w_comp, weight)
        xw = jnp.einsum('ni,rio->rno', x, rel_w)
        msg = xw[etypes, src] * norm
        node_repr = jax.ops.segment_sum(msg, dst, num_segments=x.shape[0])
        node_repr = node_repr + h_bias
        return jax.nn.relu(node_repr)
    edge_index = jnp.stack([src, dst])
    x = _layernorm(x + _L0_gnn_ref(x, edge_attr_32, L0_gnn_W1n, L0_gnn_b1n, L0_gnn_W2n, L0_gnn_b2n, L0_gnn_W1e, L0_gnn_b1e, L0_gnn_W2e, L0_gnn_b2e, L0_gnn_res_w, L0_gnn_dp_scale, L0_gnn_gamma, L0_gnn_beta, edge_index), axis=-1)
    x = _layernorm(x + _L1_gnn_ref(x, L1_gnn_weight, L1_gnn_w_comp, L1_gnn_h_bias, edge_weight1, src, dst, edge_type_8), axis=-1)
    return x

_drawn_inputs = setup_inputs


def setup_inputs(seed=0):
    import zlib

    import numpy as np

    out = dict(_drawn_inputs(seed))
    spreads = {'L0_gnn_b1n': (0.0, 0.1),
     'L0_gnn_b2n': (0.0, 0.1),
     'L0_gnn_b1e': (0.0, 0.267),
     'L0_gnn_b2e': (0.0, 0.1),
     'L0_gnn_gamma': (1.0, 0.2),
     'L0_gnn_beta': (0.0, 0.1),
     'L1_gnn_h_bias': (0.0, 0.1)}
    factors = {}
    for name, (base, spread) in spreads.items():
        noise = np.random.default_rng([zlib.crc32(name.encode()), seed]).standard_normal(out[name].shape)
        drawn = base * np.exp(spread * noise) if base else spread * noise
        out[name] = jnp.asarray(drawn.astype(out[name].dtype))
    for name, factor in factors.items():
        out[name] = (out[name] * factor).astype(out[name].dtype)
    return out
```

```python
import concourse.bass as bass
from concourse import mybir
from contextlib import ExitStack


def bass_gnn_resnorm_d2_kernel(
    nc: bass.Bass,
    x: bass.AP,
    src: bass.AP,
    dst: bass.AP,
    edge_attr: bass.AP,
    edge_type: bass.AP,
    edge_weight: bass.AP,
    W1n: bass.AP,
    b1n: bass.AP,
    W2n: bass.AP,
    b2n: bass.AP,
    W1e: bass.AP,
    b1e: bass.AP,
    W2e: bass.AP,
    b2e: bass.AP,
    res_w: bass.AP,
    dp_scale: bass.AP,
    gamma: bass.AP,
    beta: bass.AP,
    rel_basis: bass.AP,
    w_comp: bass.AP,
    h_bias: bass.AP,
    out: bass.AP,
):
    f32 = mybir.dt.float32
    bf16 = mybir.dt.bfloat16
    i32 = mybir.dt.int32
    ALU = mybir.AluOpType
    ACT = mybir.ActivationFunctionType
    AX = mybir.AxisListType

    P = 128
    N, F = x.shape
    E, DE = edge_attr.shape
    R, B = w_comp.shape
    H = W1n.shape[1]
    SLOPE, EPS = 0.1, 1e-5
    assert F == 64 and H == P and DE * 4 == P and B == 4 and 2 * F == P

    NB = -(-N // P)
    LAST_ROWS = N - (NB - 1) * P
    PAIRS = NB // 2
    assert NB == 2 * PAIRS and PAIRS % 2 == 1
    J = 4
    ST = P * J
    FULL = E // ST
    TAIL_P = (E - FULL * ST) // J
    assert TAIL_P * J == E - FULL * ST and 0 < TAIL_P < P
    GROUP = 5
    BODY = 2 * GROUP
    BODIES = FULL // BODY
    assert FULL == BODY * BODIES
    TILES = FULL + 1
    AHEAD = 3

    RC = FULL // P
    R_REST = FULL - RC * P

    node_table = nc.dram_tensor("node_table", (NB * P, F), f32, kind="Internal").ap()
    node_table2 = nc.dram_tensor("node_table2", (NB * P, F), f32, kind="Internal").ap()

    def grouped(a):
        return a[0 : FULL * ST].rearrange("(g s p j) -> g p s j", s=GROUP, p=P, j=J)

    def rest(a):
        return a[FULL * ST : E].rearrange("(p j) -> p j", j=J)

    weight_flat = edge_weight.rearrange("e o -> (e o)")
    attr_groups = edge_attr[0 : FULL * ST, :].rearrange("(g s p j) k -> g p s (j k)", s=GROUP, p=P, j=J)
    attr_rest = edge_attr[FULL * ST : E, :].rearrange("(p j) k -> p (j k)", j=J)

    ctx = ExitStack()
    with ctx:

        def sb(name, shape, dt=f32):
            return ctx.enter_context(nc.sbuf_tensor(name, shape, dt))

        def pb(name, shape, dt=f32):
            return ctx.enter_context(nc.psum_tensor(name, shape, dt))

        def sem(name):
            return ctx.enter_context(nc.semaphore(name))

        x_sb = sb("x_sb", [P, NB, F])
        acc0 = sb("acc0", [P, NB, F])
        acc1 = sb("acc1", [P, NB, 2, P])
        work = sb("work", [P, NB * F])
        xt_all = work[:, :].rearrange("p (b f) -> p b f", f=F)
        scaled = work[:, 0 : 2 * J * B * F].rearrange("p (r j b f) -> p r j b f", r=2, j=J, b=B)
        work_i = work[:, :].bitcast(i32)
        at_w = 2 * J * B * F
        is_rel = work[:, at_w : at_w + GROUP * J * R].rearrange("p (e r) -> p e r", r=R)
        at_w += GROUP * J * R
        coef_terms = work[:, at_w : at_w + GROUP * J * B * R].rearrange("p (e b r) -> p e b r", b=B, r=R)
        at_w += GROUP * J * B * R
        onehot_x = work[:, at_w : at_w + J * P].rearrange("p (j n) -> p j n", j=J)
        at_w += J * P
        onehot = work[:, at_w : at_w + 2 * J * P].rearrange("p (r j n) -> p r j n", r=2, j=J)
        dst_rows = work_i[:, 0 : RC * ST].rearrange("p (c e) -> p c e", c=RC)
        dst_rows_r = work_i[0:R_REST, RC * ST : (RC + 1) * ST]
        dst_rows_t = work_i[0:1, (RC + 1) * ST : (RC + 1) * ST + TAIL_P * J]
        at_w = (RC + 2) * ST
        b2e_parts = work[0:1, at_w : at_w + 3 * J * F // 2].bitcast(bf16).rearrange(
            "o (t j f) -> o t j f", t=3, j=J)
        rows = sb("rows", [P, BODY, J, F])
        attr = sb("attr", [P, 2, GROUP, J * DE])
        src_ix = sb("src_ix", [P, 2, GROUP * J], i32)
        dst_ix = sb("dst_ix", [P, 2, GROUP * J], i32)
        etype = sb("etype", [P, 2, GROUP * J], i32)
        enorm = sb("enorm", [P, 2, GROUP * J])
        rel = sb("rel", [P, 2, GROUP, J])
        rel_x = sb("rel_x", [P, J])
        x_pair = sb("x_pair", [P, 2, 2 * F])
        attrT = sb("attrT", [P, P])
        low = sb("low", [P, 2, 2 * P])
        hid = sb("hid", [P, 2, 2 * P])
        msg = work[:, 0 : J * F].rearrange("p (j f) -> p j f", j=J)
        coef = sb("coef", [P, 2, GROUP * J, B])

        ident = sb("ident", [P, P])
        iota_i = sb("iota_i", [P, P], i32)
        iota_f = sb("iota_f", [P, R])
        W1n_d = sb("W1n_d", [P, 2, H])
        W2n_s = sb("W2n_s", [H, F])
        b1n_c = sb("b1n_c", [H, 1])
        b1n_low = sb("b1n_low", [H, 1])
        b2n_r = sb("b2n_r", [P, F])
        W1e_d = sb("W1e_d", [P, 2, P])
        W2e_d = sb("W2e_d", [P, P])
        b1e_c = sb("b1e_c", [P, 1])
        b1e_low = sb("b1e_low", [P, 1])
        b2e_f = sb("b2e_f", [1, F])
        b2e_res = sb("b2e_res", [1, F])
        b2e_up = sb("b2e_up", [1, F])
        b2e_3 = sb("b2e_3", [3, J * F], bf16)
        ones_3 = sb("ones_3", [3, P], bf16)
        gamma_r = sb("gamma_r", [P, F])
        beta_r = sb("beta_r", [P, F])
        hbias_r = sb("hbias_r", [P, F])
        res_c = sb("res_c", [P, 1])
        dp_c = sb("dp_c", [P, 1])
        scale_c = sb("scale_c", [P, 1])
        basis = sb("basis", [P, 2, F])
        wcomp_r = sb("wcomp_r", [P, R, B])
        RCH = RC + 2
        spans_i = sb("spans_i", [P, RCH, 2], i32)
        spans = sb("spans", [P, RCH, 2])
        base = sb("base", [P, TILES])
        control = sb("control", [1, TILES, 2], i32)
        CH = 14
        CHUNKS = NB // CH
        CH2 = 7
        CHUNKS2 = NB // CH2
        mean = sb("mean", [P, NB])
        var = sb("var", [P, NB])
        std = sb("std", [P, NB])
        rstd = sb("rstd", [P, NB])

        ps_T = pb("ps_T", [P, P])
        ps_z = [pb(f"ps_z{k}", [P, 512]) for k in range(2)]
        ps_o = [pb(f"ps_o{k}", [P, 512]) for k in range(2)]
        ps_agg = [pb(f"ps_agg{k}", [P, 512]) for k in range(2)]
        ps_iota = pb("ps_iota", [P, 512])

        s_const = sem("s_const")
        s_x = sem("s_x")
        s_rows = sem("s_rows")
        s_pool = sem("s_pool")
        s_zero = sem("s_zero")
        s_b2e = sem("s_b2e")
        s_b2e3 = sem("s_b2e3")
        s_setup = sem("s_setup")
        s_spans = sem("s_spans")
        s_bcast = sem("s_bcast")
        s_control = sem("s_control")
        s_dve = sem("s_dve")
        node_staged = sem("node_staged")
        node_T = sem("node_T")
        node_copied = sem("node_copied")
        node_mm1 = sem("node_mm1")
        node_low = sem("node_low")
        node_hid = sem("node_hid")
        node_mm2 = sem("node_mm2")
        node_out = sem("node_out")
        table_ready = sem("table_ready")
        table2_ready = sem("table2_ready")
        s_out = sem("s_out")

        attr_loaded = [sem(f"attr_loaded{h}") for h in range(2)]
        src_loaded = [[sem(f"src_loaded{l}{h}") for h in range(2)] for l in range(2)]
        dst_loaded = [[sem(f"dst_loaded{l}{h}") for h in range(2)] for l in range(2)]
        type_loaded = [sem(f"type_loaded{h}") for h in range(2)]
        norm_loaded = [sem(f"norm_loaded{h}") for h in range(2)]
        gathered = [[sem(f"gathered{l}_{u}") for u in range(BODY)] for l in range(2)]
        transposed = sem("transposed")
        attr_copied = sem("attr_copied")
        mm1_done = sem("mm1_done")
        low_ready = sem("low_ready")
        hid_ready = sem("hid_ready")
        mm2_done = sem("mm2_done")
        msg_ready = [sem("msg_ready"), sem("scaled_ready")]
        rel_ready = [sem(f"rel_ready{l}") for l in range(2)]
        coef_ready = sem("coef_ready")
        rel_moved = [sem(f"rel_moved{l}") for l in range(2)]
        s_link = sem("s_link")
        gathers_begun = sem("gathers_begun")
        all_added = sem("all_added")
        onehot_ready = [sem(f"onehot_ready{l}") for l in range(2)]
        scattered = [sem(f"scattered{l}") for l in range(2)]
        added = [sem(f"added{l}") for l in range(2)]
        x_onehot_ready = [sem(f"x_onehot_ready{l}") for l in range(2)]
        x_scattered = [sem(f"x_scattered{l}") for l in range(2)]
        x_added = [sem(f"x_added{l}") for l in range(2)]
        centered = sem("centered")
        squared = sem("squared")
        var_ready = sem("var_ready")
        std_ready = sem("std_ready")
        normed = sem("normed")
        transformed = sem("transformed")
        bias_added = sem("bias_added")
        normed2 = sem("normed2")

        block = ctx.enter_context(nc.Block())

        def tile_of(i, u):
            return i * BODY + u

        def slot_of(u):
            return u % BODY

        def half_of(u):
            return (u % BODY) // GROUP

        def uses(i, u):
            return i + (u // BODY) + 1

        def const_loads(sp):
            n = 0

            def ld(o, i):
                nonlocal n
                sp.dma_start(o, i).then_inc(s_const, 16)
                n += 1

            ld(W1n_d[0:F, 0, :], W1n)
            ld(W1n_d[F:P, 1, :], W1n)
            ld(W2n_s[:], W2n)
            ld(b1n_c[:], b1n.rearrange("(p o) -> p o", o=1))
            ld(b2n_r[:], b2n.rearrange("(o f) -> o f", o=1).to_broadcast([P, F]))
            for pr in range(2):
                for h in range(2):
                    at = (2 * pr + h) * DE
                    ld(W1e_d[at : at + DE, pr, h * F : h * F + F], W1e)
            ld(W2e_d[0:F, 0:F], W2e)
            ld(W2e_d[F:P, F:P], W2e)
            b1e_v = b1e.rearrange("(p o) -> p o", o=1)
            ld(b1e_c[0:F, :], b1e_v)
            ld(b1e_c[F:P, :], b1e_v)
            ld(b2e_f[:], b2e.rearrange("(o f) -> o f", o=1))
            ld(gamma_r[:], gamma.rearrange("(o f) -> o f", o=1).to_broadcast([P, F]))
            ld(beta_r[:], beta.rearrange("(o f) -> o f", o=1).to_broadcast([P, F]))
            ld(hbias_r[:], h_bias.rearrange("(o f) -> o f", o=1).to_broadcast([P, F]))
            ld(res_c[:], res_w.rearrange("(o f) -> o f", o=1).to_broadcast([P, 1]))
            ld(dp_c[:], dp_scale.rearrange("(o f) -> o f", o=1).to_broadcast([P, 1]))
            ld(basis[:], rel_basis.rearrange("(q b) i o -> (b i) q o", q=2))
            ld(
                wcomp_r[:].rearrange("p r b -> p (r b)"),
                w_comp.rearrange("(o r) b -> o (r b)", o=1).to_broadcast([P, R * B]),
            )
            return n

        CONST_LOADS = 21
        NODE_STORES = PAIRS // 2 + 1
        MID_STORES = CHUNKS
        ALL_GATHERS = 16 * J

        @block.sync
        def _(sp):
            x_main = x[0 : (NB - 1) * P, :].rearrange("(b p) f -> p b f", p=P)
            cut = 16
            sp.dma_start(x_sb[:, 0:cut, :], x_main[:, 0:cut, :]).then_inc(s_x, 16)
            sp.wait_ge(s_zero, 4)
            n = const_loads(sp)
            assert n == CONST_LOADS, n
            sp.dma_start(x_sb[:, cut : NB - 1, :], x_main[:, cut:, :]).then_inc(s_rows, 16)
            sp.dma_start(x_sb[0:LAST_ROWS, NB - 1, :], x[(NB - 1) * P : N, :]).then_inc(s_rows, 16)
            sp.dma_start(
                dst_rows, dst[0 : RC * P * ST].rearrange("(c p e) -> p c e", c=RC, p=P)
            ).then_inc(s_rows, 16)
            sp.dma_start(
                dst_rows_r, dst[RC * P * ST : FULL * ST].rearrange("(p e) -> p e", e=ST)
            ).then_inc(s_rows, 16)
            sp.dma_start(
                dst_rows_t, dst[FULL * ST : E].rearrange("(o e) -> o e", o=1)
            ).then_inc(s_rows, 16)
            sp.wait_ge(s_b2e, 1)
            sp.dma_start(b2e_3[:], b2e_parts.rearrange("o t j f -> o t (j f)")).then_inc(s_b2e3, 16)

            def load_group(l, h, g):
                sp.dma_start(
                    src_ix[:, h, :].rearrange("p (s j) -> p s j", j=J), grouped(src)[g]
                ).then_inc(src_loaded[l][h], 16)
                sp.dma_start(
                    dst_ix[:, h, :].rearrange("p (s j) -> p s j", j=J), grouped(dst)[g]
                ).then_inc(dst_loaded[l][h], 16)
                if l == 0:
                    sp.dma_start(attr[:, h, :, :], attr_groups[g]).then_inc(attr_loaded[h], 16)
                else:
                    sp.dma_start(
                        etype[:, h, :].rearrange("p (s j) -> p s j", j=J), grouped(edge_type)[g]
                    ).then_inc(type_loaded[h], 16)
                    sp.dma_start(
                        enorm[:, h, :].rearrange("p (s j) -> p s j", j=J), grouped(weight_flat)[g]
                    ).then_inc(norm_loaded[h], 16)

            def load_tail(l):
                sp.dma_start(src_ix[0:TAIL_P, 0, 0:J], rest(src)).then_inc(src_loaded[l][0], 16)
                sp.dma_start(dst_ix[0:TAIL_P, 0, 0:J], rest(dst)).then_inc(dst_loaded[l][0], 16)
                if l == 0:
                    sp.dma_start(attr[0:TAIL_P, 0, 0, :], attr_rest).then_inc(attr_loaded[0], 16)
                else:
                    sp.dma_start(etype[0:TAIL_P, 0, 0:J], rest(edge_type)).then_inc(type_loaded[0], 16)
                    sp.dma_start(enorm[0:TAIL_P, 0, 0:J], rest(weight_flat)).then_inc(norm_loaded[0], 16)

            def layer_loads(l):
                with sp.Fori(0, BODIES - 1) as i:
                    for h in range(2):
                        sp.wait_ge(msg_ready[l], i * BODY + (h + 1) * GROUP)
                        load_group(l, h, i * 2 + (2 + h))
                sp.wait_ge(msg_ready[l], (BODIES - 1) * BODY + GROUP)
                load_tail(l)

            for h in range(2):
                load_group(0, h, h)
            table_v = node_table[0 : (NB - 2) * P, :].rearrange("(i b p) f -> i p b f", b=4, p=P)
            with sp.Fori(0, PAIRS // 2) as i:
                sp.wait_ge(node_out, i * 2 + 2)
                sp.dma_start(table_v[i], xt_all[:, bass.ds(i * 4, 4), :]).then_inc(table_ready, 16)
            sp.wait_ge(node_out, PAIRS)
            sp.dma_start(
                node_table[(NB - 2) * P :, :].rearrange("(b p) f -> p b f", p=P), xt_all[:, NB - 2 :, :]
            ).then_inc(table_ready, 16)
            layer_loads(0)
            sp.wait_ge(msg_ready[0], TILES)
            for h in range(2):
                load_group(1, h, h)
            for c in range(CHUNKS):
                sp.wait_ge(normed, c + 1)
                sp.dma_start(
                    node_table2[c * CH * P : (c + 1) * CH * P, :].rearrange("(b p) f -> p b f", p=P),
                    x_sb[:, c * CH : (c + 1) * CH, :],
                ).then_inc(table2_ready, 16)
            layer_loads(1)
            for c in range(CHUNKS2):
                sp.wait_ge(normed2, c + 1)
                lo, hi = c * CH2, min((c + 1) * CH2, NB - 1)
                sp.dma_start(
                    out[lo * P : hi * P, :].rearrange("(b p) f -> p b f", p=P), x_sb[:, lo:hi, :]
                ).then_inc(s_out, 16)
            sp.dma_start(out[(NB - 1) * P : N, :], x_sb[0:LAST_ROWS, NB - 1, :]).then_inc(s_out, 16)
            sp.wait_ge(s_out, 16 * (CHUNKS2 + 1))

        @block.gpsimd
        def _(pool):
            nc.gpsimd.memset(W1n_d[:], 0.0).then_inc(s_zero, 1)
            nc.gpsimd.memset(W1e_d[:], 0.0).then_inc(s_zero, 1)
            nc.gpsimd.memset(W2e_d[:], 0.0).then_inc(s_zero, 1)
            nc.gpsimd.memset(x_sb[:, NB - 1, :], 0.0).then_inc(s_zero, 1)
            nc.gpsimd.memset(ident[:], 0.0).then_inc(s_pool, 1)
            nc.gpsimd.iota(iota_i[:], pattern=[[1, P]], base=0, channel_multiplier=0).then_inc(s_pool, 1)
            pool.wait_ge(s_pool, 2)
            nc.gpsimd.affine_select(
                out=ident[:], in_=ident[:], compare_op=ALU.not_equal, fill=1.0, base=0,
                pattern=[[-1, P]], channel_multiplier=1,
            ).then_inc(s_pool, 1)
            nc.gpsimd.memset(ones_3[:], 1.0).then_inc(s_pool, 1)

            def stage(q, k):
                pool.wait_ge(s_rows, 16 * 5)
                nc.gpsimd.tensor_copy(
                    x_pair[:, k, :], x_sb[:, bass.ds(q * 2, 2), :].rearrange("p b f -> p (b f)")
                ).then_inc(node_staged, 1)

            pool.wait_ge(s_x, 16)
            for q in range(3):
                if q == 2:
                    pool.wait_ge(node_T, 1)
                stage(q, q % 2)
            with pool.Fori(1, PAIRS // 2) as i:
                for k in range(2):
                    pool.wait_ge(node_T, i * 2 + k)
                    stage(i * 2 + (k + 1), 1 - k)
            nc.gpsimd.memset(acc0[:], 0.0).then_inc(s_pool, 1)
            nc.gpsimd.memset(acc1[:], 0.0).then_inc(s_pool, 1)

            def gather(l, i, u, slot_used=None):
                table = (node_table, node_table2)[l]
                if slot_used is not None:
                    pool.wait_ge(msg_ready[l], slot_used)
                if (u % GROUP) == 0:
                    pool.wait_ge(src_loaded[l][half_of(u)], uses(i, u) * 16)
                pool.sem_inc(gathers_begun, 1)
                for j in range(J):
                    col = (u % GROUP) * J + j
                    nc.gpsimd.indirect_dma_start(
                        rows[:, slot_of(u), j, :], None, table,
                        bass.IndirectOffsetOnAxis(ap=src_ix[:, half_of(u), col : col + 1], axis=0),
                    ).then_inc(gathered[l][slot_of(u)], 16)

            for l in range(2):
                ready, count = ((table_ready, 16 * NODE_STORES), (table2_ready, 16 * MID_STORES))[l]
                pool.wait_ge(ready, count)
                for u in range(BODY):
                    gather(l, 0, u)
                with pool.Fori(1, BODIES) as i:
                    for u in range(BODY):
                        gather(l, i, u, i * BODY + (u + 1 - BODY))
                gather(l, BODIES, 0, FULL + 1 - BODY)

        @block.scalar
        def _(act):
            act.wait_ge(s_const, 16 * CONST_LOADS)
            nc.scalar.mul(b1n_low[:], b1n_c[:], SLOPE).then_inc(s_setup, 1)
            nc.scalar.mul(b1e_low[:], b1e_c[:], SLOPE).then_inc(s_setup, 1)
            act.wait_ge(s_setup, 2)

            def node_copy(q):
                act.wait_ge(node_T, q + 1)
                nc.scalar.copy(attrT[:], ps_T[:]).then_inc(node_copied, 1)

            def node_lower(q, k):
                act.wait_ge(node_mm1, q + 1)
                nc.scalar.activation(
                    low[:, k, :], ps_z[k][:, 0 : 2 * P], ACT.Identity, bias=b1n_low[:], scale=SLOPE
                ).then_inc(node_low, 1)

            node_copy(0)
            with act.Fori(0, PAIRS // 2) as i:
                for k in range(2):
                    node_copy(i * 2 + (k + 1))
                    node_lower(i * 2 + k, k)
            node_lower(PAIRS - 1, 0)

            def edge_copy(i, u):
                act.wait_ge(transposed, tile_of(i, u) + 1)
                nc.scalar.copy(attrT[:], ps_T[:]).then_inc(attr_copied, 1)

            def edge_lower(i, u):
                act.wait_ge(mm1_done, tile_of(i, u) + 1)
                nc.scalar.activation(
                    low[:, 0, :], ps_z[0][:, 0 : 2 * P], ACT.Identity, bias=b1e_low[:], scale=SLOPE
                ).then_inc(low_ready, 1)

            def step(i, u, last=TILES):
                if last is None or i * BODY + u + 1 < TILES:
                    edge_lower(i, u + 1)
                if last is None or i * BODY + u + 2 < TILES:
                    edge_copy(i, u + 2)

            edge_copy(0, 0)
            edge_lower(0, 0)
            edge_copy(0, 1)
            with act.Fori(0, BODIES - 1) as i:
                for u in range(BODY):
                    step(i, u, None)
            for u in range(BODY + 1):
                step(BODIES - 1, u)

            def square(k, count, cols):
                act.wait_ge(centered, count)
                nc.scalar.activation(work[:, cols], acc0[:, :, :].rearrange("p b f -> p (b f)")[:, cols],
                                     ACT.Square).then_inc(squared, 1)

            def root(count, blocks):
                act.wait_ge(var_ready, count)
                nc.scalar.activation(std[:, blocks], var[:, blocks], ACT.Sqrt).then_inc(std_ready, 1)

            def chunk(c, n):
                return slice(c * n * F, (c + 1) * n * F), slice(c * n, (c + 1) * n)

            n = 0
            for c in range(CHUNKS):
                for norm in range(2):
                    n += 1
                    cols, blocks = chunk(c, CH)
                    square(0, n, cols)
                    root(n, blocks)
            for c in range(CHUNKS2):
                n += 1
                cols, blocks = chunk(c, CH2)
                square(0, n, cols)
                root(n, blocks)

        @block.vector
        def _(dve):
            steps = [0]

            def link(ins):
                steps[0] += 1
                ins.then_inc(s_dve, 1)
                dve.wait_ge(s_dve, steps[0])

            dve.wait_ge(s_pool, 2)
            nc.vector.tensor_copy(ps_iota[:, 0:P], iota_i[:])
            nc.vector.tensor_copy(iota_f[:], iota_i[:, 0:R])
            link(nc.vector.memset(spans_i[:], 0))
            dve.wait_ge(s_const, 16 * CONST_LOADS)
            link(nc.vector.tensor_tensor(scale_c[:], res_c[:], dp_c[:], ALU.mult))
            rest_of = b2e_f
            for t in range(3):
                part = b2e_parts[:, t, :, :]
                link(nc.vector.tensor_copy(part, rest_of[:].rearrange("o (j f) -> o j f", j=1).to_broadcast([1, J, F])))
                if t < 2:
                    link(nc.vector.tensor_copy(b2e_up[:], b2e_parts[:, t, 0, :]))
                    link(nc.vector.tensor_tensor(b2e_res[:], rest_of[:], b2e_up[:], ALU.subtract))
                    rest_of = b2e_res
            dve.sem_inc(s_b2e, 1)

            dve.wait_ge(s_rows, 16 * 5)
            for v, op in enumerate((ALU.min, ALU.max)):
                nc.vector.tensor_reduce(spans_i[:, 0:RC, v], dst_rows, axis=AX.X, op=op)
                nc.vector.tensor_reduce(spans_i[0:R_REST, RC, v : v + 1], dst_rows_r, axis=AX.X, op=op)
                link(nc.vector.tensor_reduce(spans_i[0:1, RC + 1, v : v + 1], dst_rows_t, axis=AX.X, op=op))
            link(nc.vector.tensor_scalar(spans_i[:], spans_i[:], 7, None, ALU.logical_shift_right))
            link(nc.vector.tensor_copy(spans[:], spans_i[:]))
            nc.vector.tensor_tensor(
                spans[:, :, 1], spans[:, :, 1], spans[:, :, 0], ALU.subtract
            ).then_inc(s_spans, 1)
            dve.wait_ge(s_bcast, 1)
            nc.vector.tensor_scalar(base[:], ps_agg[0][:, 0:TILES], float(P), None, ALU.mult)
            nc.vector.tensor_copy(control[:, :, 0], ps_agg[0][0:1, 0:TILES])
            nc.vector.tensor_copy(control[:, :, 1], ps_agg[1][0:1, 0:TILES]).then_inc(s_control, 1)
            dve.wait_ge(s_control, 1)

            def node_hidden(q, k):
                dve.wait_ge(node_low, q + 1)
                nc.vector.scalar_tensor_tensor(
                    hid[:, k, :], ps_z[k][:, 0 : 2 * P], b1n_c[:], low[:, k, :], ALU.add, ALU.max
                ).then_inc(node_hid, 1)

            def node_store(q, k):
                dve.wait_ge(node_mm2, q + 1)
                nc.vector.tensor_tensor(
                    xt_all[:, bass.ds(q * 2, 2), :],
                    ps_o[k][:, 0 : 2 * F].rearrange("p (b f) -> p b f", b=2),
                    b2n_r[:].rearrange("p (o f) -> p o f", o=1).to_broadcast([P, 2, F]),
                    ALU.add,
                ).then_inc(node_out, 1)

            dve.wait_ge(s_b2e3, 16)
            node_hidden(0, 0)
            with dve.Fori(0, PAIRS // 2) as i:
                for k in range(2):
                    node_hidden(i * 2 + (k + 1), 1 - k)
                    node_store(i * 2 + k, k)
            node_store(PAIRS - 1, 0)

            first, further, k_reg, x_done = (
                dve.alloc_register(f"dve_{n}") for n in ("first", "further", "k", "x_done")
            )

            def relative(l, i, u):
                h = half_of(u)
                dve.wait_ge(dst_loaded[l][h], uses(i, u) * 16)
                s = tile_of(i, u)
                nc.vector.tensor_tensor(
                    rel[:, h, :, :],
                    dst_ix[:, h, :].rearrange("p (s j) -> p s j", j=J),
                    base[:, bass.ds(s, GROUP)].rearrange("p (s o) -> p s o", o=1).to_broadcast([P, GROUP, J]),
                    ALU.subtract,
                ).then_inc(rel_ready[l], 1)

            def relative_tail(l):
                dve.wait_ge(dst_loaded[l][0], (BODIES + 1) * 16)
                link(nc.vector.memset(rel[:, 0, 0, :], -1.0))
                nc.vector.tensor_tensor(
                    rel[0:TAIL_P, 0, 0, :],
                    dst_ix[0:TAIL_P, 0, 0:J],
                    base[0:TAIL_P, FULL : FULL + 1].to_broadcast([TAIL_P, J]),
                    ALU.subtract,
                ).then_inc(rel_ready[l], 1)

            def one_hot(o, r, done, wait, count):
                dve.wait_ge(wait, count)
                nc.vector.tensor_tensor(
                    o,
                    ps_iota[:, 0:P].rearrange("p (o n) -> p o n", o=1).to_broadcast([P, J, P]),
                    r.rearrange("p (j o) -> p j o", o=1).to_broadcast([P, J, P]),
                    ALU.is_equal,
                ).then_inc(done, 1)

            def main_one_hot(l, i, u, ring):
                group_no = i * 2 + (u // GROUP) + 1
                one_hot(onehot[:, ring, :, :], rel[:, half_of(u), u % GROUP, :], onehot_ready[l],
                        rel_ready[l], group_no)

            def sums_at(l, blk):
                if l == 0:
                    return acc0[:, bass.ds(blk, 1), :].rearrange("p o f -> p (o f)")
                return acc1[:, bass.ds(blk, 1), :, :].rearrange("p o q n -> p (o q n)")

            width = (F, 2 * P)

            def add_sums(l, i, u, bank):
                s = tile_of(i, u)
                dve.wait_ge(added[l], s)
                dve.wait_ge(scattered[l], s + 1)
                a = sums_at(l, dve.snap(first))
                nc.vector.tensor_tensor(a, a, bank[:, 0 : width[l]], ALU.add).then_inc(added[l], 1)

            def extras(l, i, u, bank):
                s = tile_of(i, u)
                dve.reg_mov(k_reg, 0)
                with dve.While(lambda: dve.snap(k_reg) < dve.snap(further)):
                    with_prev = rel[:, half_of(u), u % GROUP, :]
                    dve.wait_ge(added[l], s + 1)
                    nc.vector.tensor_scalar(with_prev, with_prev, float(P), None, ALU.subtract).then_inc(
                        rel_moved[l], 1
                    )
                    dve.reg_add(x_done, x_done, 1)
                    one_hot(onehot_x, with_prev, x_onehot_ready[l], rel_moved[l], dve.snap(x_done))
                    dve.wait_ge(x_scattered[l], dve.snap(x_done))
                    a = sums_at(l, dve.snap(first) + dve.snap(k_reg) + 1)
                    nc.vector.tensor_tensor(a, a, bank[:, 0 : width[l]], ALU.add).then_inc(x_added[l], 1)
                    dve.wait_ge(x_added[l], dve.snap(x_done))
                    dve.reg_add(k_reg, k_reg, 1)

            def spans_of(i, u):
                dve.reg_load(
                    [first, further],
                    control[0:1, bass.ds(tile_of(i, u), 1), :].rearrange("p o v -> p (o v)"),
                )

            def edge_hidden(i, u):
                dve.wait_ge(low_ready, tile_of(i, u) + 1)
                nc.vector.scalar_tensor_tensor(
                    hid[:, 0, :], ps_z[0][:, 0 : 2 * P], b1e_c[:], low[:, 0, :], ALU.add, ALU.max
                ).then_inc(hid_ready, 1)

            def message(i, u):
                dve.wait_ge(gathered[0][slot_of(u)], uses(i, u) * ALL_GATHERS)
                dve.wait_ge(mm2_done, tile_of(i, u) + 1)
                nc.vector.tensor_tensor(
                    msg.rearrange("p j f -> p (j f)"),
                    ps_o[0][:, 0 : J * F],
                    rows[:, slot_of(u), :, :].rearrange("p j f -> p (j f)"),
                    ALU.mult,
                ).then_inc(msg_ready[0], 1)

            def step0(i, u, tail=False):
                spans_of(i, u)
                if tail and i * BODY + u == FULL:
                    relative_tail(0)
                elif u % GROUP == 0:
                    relative(0, i, u)
                main_one_hot(0, i, u, 0)
                message(i, u)
                if not (tail and i * BODY + u + 1 >= TILES):
                    edge_hidden(i, u + 1)
                add_sums(0, i, u, ps_agg[0])
                extras(0, i, u, ps_agg[1])

            dve.wait_ge(s_pool, 6)
            dve.wait_ge(table_ready, 16 * NODE_STORES)
            dve.reg_mov(x_done, 0)
            edge_hidden(0, 0)
            with dve.Fori(0, BODIES - 1) as i:
                for u in range(BODY):
                    step0(i, u)
            for u in range(BODY + 1):
                step0(BODIES - 1, u, tail=True)

            o_all = acc0[:, :, :].rearrange("p b f -> p (b f)")
            x_all = x_sb[:, :, :].rearrange("p b f -> p (b f)")

            def blocks_of(c, n):
                return slice(c * n * F, (c + 1) * n * F), slice(c * n, (c + 1) * n)

            def by_block(ap, n):
                return ap.rearrange("p (b f) -> p b f", f=F)

            def over_features(ap, n):
                return ap.rearrange("p (b o) -> p b o", o=1).to_broadcast([P, n, F])

            def over_blocks(ap, n):
                return ap.rearrange("p (o f) -> p o f", o=1).to_broadcast([P, n, F])

            def center(c, n):
                cols, bl = blocks_of(c, n)
                o = by_block(o_all[:, cols], n)
                link(nc.vector.tensor_reduce(mean[:, bl], o, axis=AX.X, op=ALU.add))
                link(nc.vector.tensor_scalar(mean[:, bl], mean[:, bl], 1.0 / F, None, ALU.mult))
                nc.vector.tensor_tensor(o, o, over_features(mean[:, bl], n), ALU.subtract).then_inc(centered, 1)

            def variance(c, n, count):
                cols, bl = blocks_of(c, n)
                dve.wait_ge(squared, count)
                link(nc.vector.tensor_reduce(var[:, bl], by_block(work[:, cols], n), axis=AX.X, op=ALU.add))
                nc.vector.tensor_scalar(var[:, bl], var[:, bl], 1.0 / F, EPS, ALU.mult, ALU.add).then_inc(
                    var_ready, 1
                )

            def by_std(o, c, n, count, target):
                cols, bl = blocks_of(c, n)
                dve.wait_ge(std_ready, count)
                link(nc.vector.reciprocal(rstd[:, bl], std[:, bl]))
                return nc.vector.tensor_tensor(target, o, over_features(rstd[:, bl], n), ALU.mult)

            n_norm = 0
            for c in range(CHUNKS):
                cols, bl = blocks_of(c, CH)
                o = by_block(o_all[:, cols], CH)
                if c == 0:
                    dve.wait_ge(added[0], TILES)
                link(nc.vector.scalar_tensor_tensor(
                    o_all[:, cols], o_all[:, cols], scale_c[:], x_all[:, cols], ALU.mult, ALU.add))
                center(c, CH)
                n_norm += 1
                variance(c, CH, n_norm)
                link(by_std(o, c, CH, n_norm, o))
                link(nc.vector.tensor_tensor(o, o, over_blocks(gamma_r[:], CH), ALU.mult))
                link(nc.vector.tensor_tensor(o, o, over_blocks(beta_r[:], CH), ALU.add))
                link(nc.vector.tensor_tensor(o_all[:, cols], o_all[:, cols], x_all[:, cols], ALU.add))
                center(c, CH)
                n_norm += 1
                variance(c, CH, n_norm)
                by_std(o, c, CH, n_norm, by_block(x_all[:, cols], CH)).then_inc(normed, 1)

            def coefficients(i, u, rows_p=P, cols=GROUP * J):
                h = half_of(u)
                dve.wait_ge(type_loaded[h], uses(i, u) * 16)
                link_l(nc.vector.tensor_tensor(
                    is_rel,
                    etype[:, h, :].rearrange("p (e o) -> p e o", o=1).to_broadcast([P, GROUP * J, R]),
                    iota_f[:].rearrange("p (o r) -> p o r", o=1).to_broadcast([P, GROUP * J, R]),
                    ALU.is_equal))
                dve.wait_ge(norm_loaded[h], uses(i, u) * 16)
                link_l(nc.vector.tensor_tensor(
                    is_rel, is_rel,
                    enorm[:, h, :].rearrange("p (e o) -> p e o", o=1).to_broadcast([P, GROUP * J, R]),
                    ALU.mult))
                link_l(nc.vector.tensor_tensor(
                    coef_terms,
                    is_rel.rearrange("p e (o r) -> p e o r", o=1).to_broadcast([P, GROUP * J, B, R]),
                    wcomp_r[:].rearrange("p r b -> p b r").rearrange("p (o b) r -> p o b r", o=1).to_broadcast([P, GROUP * J, B, R]),
                    ALU.mult))
                nc.vector.tensor_reduce(coef[:, h, :, :], coef_terms, axis=AX.X, op=ALU.add).then_inc(
                    coef_ready, 1)

            l_steps = dve.alloc_register("dve_link")
            dve.reg_mov(l_steps, 0)

            def link_l(ins):
                ins.then_inc(s_link, 1)
                dve.reg_add(l_steps, l_steps, 1)
                dve.wait_ge(s_link, dve.snap(l_steps))

            def scale_rows(i, u, ring):
                dve.wait_ge(coef_ready, i * 2 + (u // GROUP) + 1)
                dve.wait_ge(gathered[1][slot_of(u)], uses(i, u) * ALL_GATHERS)
                h, at = half_of(u), (u % GROUP) * J
                nc.vector.tensor_tensor(
                    scaled[:, ring, :, :, :],
                    rows[:, slot_of(u), :, :].rearrange("p j (o f) -> p j o f", o=1).to_broadcast([P, J, B, F]),
                    coef[:, h, at : at + J, :].rearrange("p j (b o) -> p j b o", o=1).to_broadcast([P, J, B, F]),
                    ALU.mult,
                ).then_inc(msg_ready[1], 1)

            def prepare1(i, u, tail=False):
                if tail:
                    relative_tail(1)
                    coefficients(i, u)
                elif u % GROUP == 0:
                    relative(1, i, u)
                    coefficients(i, u)
                main_one_hot(1, i, u, u % 2)
                scale_rows(i, u, u % 2)

            def finish1(i, u):
                spans_of(i, u)
                add_sums(1, i, u, ps_agg[u % 2])
                extras(1, i, u, ps_z[0])

            dve.reg_mov(x_done, 0)
            prepare1(0, 0)
            with dve.Fori(0, BODIES - 1) as i:
                for u in range(BODY):
                    prepare1(i, u + 1)
                    finish1(i, u)
            for u in range(BODY + 1):
                if u < BODY:
                    prepare1(BODIES - 1, u + 1, tail=(u + 1 == BODY))
                finish1(BODIES - 1, u)
            dve.wait_ge(added[1], TILES)
            nc.vector.memset(spans_i[0:1, 0, :], 0).then_inc(all_added, 1)

            for c in range(CHUNKS2):
                cols, bl = blocks_of(c, CH2)
                o = by_block(o_all[:, cols], CH2)
                dve.wait_ge(transformed, c + 1)
                nc.vector.tensor_tensor(
                    o, by_block(ps_o[c % 2][:, 0 : CH2 * F], CH2), over_blocks(hbias_r[:], CH2), ALU.add
                ).then_inc(bias_added, 1)
                dve.wait_ge(bias_added, c + 1)
                link(nc.vector.scalar_tensor_tensor(
                    o_all[:, cols], o_all[:, cols], 0.0, x_all[:, cols], ALU.max, ALU.add))
                center(c, CH2)
                n_norm += 1
                variance(c, CH2, n_norm)
                by_std(o, c, CH2, n_norm, by_block(x_all[:, cols], CH2)).then_inc(normed2, 1)

        @block.tensor
        def _(pe):
            pe.wait_ge(s_pool, 4)
            pe.wait_ge(s_spans, 1)
            for v in range(2):
                for c in range(RCH):
                    rows_c = (P, R_REST, 1)[max(0, c - RC + 1)]
                    at = FULL if c == RCH - 1 else c * P
                    last = nc.tensor.matmul(
                        ps_agg[v][:, at : at + rows_c],
                        spans[0:rows_c, c, v : v + 1].to_broadcast([rows_c, P]),
                        ident[0:rows_c, 0:rows_c], start=True, stop=True,
                    )
            last.then_inc(s_bcast, 1)

            def node_transpose(q, k):
                pe.wait_ge(node_staged, q + 1)
                nc.tensor.transpose(ps_T[:], x_pair[:, k, :], ident[:]).then_inc(node_T, 1)

            def node_first(q, k):
                pe.wait_ge(node_copied, q + 1)
                for b in range(2):
                    last = nc.tensor.matmul(
                        ps_z[k][:, b * P : (b + 1) * P], W1n_d[:, b, :], attrT[:], start=True, stop=True
                    )
                last.then_inc(node_mm1, 1)

            def node_second(q, k):
                pe.wait_ge(node_hid, q + 1)
                for b in range(2):
                    last = nc.tensor.matmul(
                        ps_o[k][:, b * F : (b + 1) * F], hid[:, k, b * P : (b + 1) * P], W2n_s[:],
                        start=True, stop=True,
                    )
                last.then_inc(node_mm2, 1)

            pe.wait_ge(s_const, 16 * CONST_LOADS)
            pe.wait_ge(s_x, 16)
            node_transpose(0, 0)
            node_first(0, 0)
            node_transpose(1, 1)
            with pe.Fori(0, PAIRS // 2 - 1) as i:
                for k in range(2):
                    node_first(i * 2 + (k + 1), 1 - k)
                    node_transpose(i * 2 + (k + 2), k)
                    node_second(i * 2 + k, k)
            node_first(PAIRS - 2, 1)
            node_transpose(PAIRS - 1, 0)
            node_second(PAIRS - 3, 0)
            node_first(PAIRS - 1, 0)
            node_second(PAIRS - 2, 1)
            node_second(PAIRS - 1, 0)

            further, k_reg, x_done = (pe.alloc_register(f"pe_{n}") for n in ("further", "k", "x_done"))

            def attr_transpose(i, u):
                if u % GROUP == 0:
                    pe.wait_ge(attr_loaded[half_of(u)], uses(i, u) * 16)
                nc.tensor.transpose(ps_T[:], attr[:, half_of(u), u % GROUP, :], ident[:]).then_inc(
                    transposed, 1
                )

            def edge_first(i, u):
                pe.wait_ge(attr_copied, tile_of(i, u) + 1)
                for pr in range(2):
                    last = nc.tensor.matmul(
                        ps_z[0][:, pr * P : (pr + 1) * P], W1e_d[:, pr, :], attrT[:], start=True, stop=True
                    )
                last.then_inc(mm1_done, 1)

            def edge_second(i, u):
                pe.wait_ge(hid_ready, tile_of(i, u) + 1)
                nc.tensor.matmul(
                    ps_o[0][:, 0 : J * F], ones_3[:], b2e_3[:], start=True, stop=False, skip_group_check=True
                )
                for pr in range(2):
                    last = nc.tensor.matmul(
                        ps_o[0][:, pr * P : (pr + 1) * P], hid[:, 0, pr * P : (pr + 1) * P], W2e_d[:],
                        start=False, stop=(pr == 1), skip_group_check=True,
                    )
                last.then_inc(mm2_done, 1)

            def sum_by_target(l, hot, bank, ring):
                if l == 0:
                    for j in range(J):
                        last = nc.tensor.matmul(
                            bank[:, 0:F], hot[:, j, :], msg[:, j, :], start=(j == 0), stop=(j == J - 1)
                        )
                    return last
                for pr in range(2):
                    for j in range(J):
                        last = nc.tensor.matmul(
                            bank[:, pr * P : (pr + 1) * P],
                            scaled[:, ring, j, 2 * pr : 2 * pr + 2, :].rearrange("p b f -> p (b f)"),
                            hot[:, j, :], start=(j == 0), stop=(j == J - 1),
                        )
                return last

            def scatter(l, i, u, ring, bank, bank_x):
                s = tile_of(i, u)
                pe.reg_load(further, control[0:1, bass.ds(s, 1), 1:2].rearrange("p o v -> p (o v)"))
                pe.wait_ge(onehot_ready[l], s + 1)
                pe.wait_ge(msg_ready[l], s + 1)
                sum_by_target(l, onehot[:, ring, :, :], bank, ring).then_inc(scattered[l], 1)
                pe.reg_mov(k_reg, 0)
                with pe.While(lambda: pe.snap(k_reg) < pe.snap(further)):
                    pe.reg_add(k_reg, k_reg, 1)
                    pe.reg_add(x_done, x_done, 1)
                    pe.wait_ge(x_onehot_ready[l], pe.snap(x_done))
                    sum_by_target(l, onehot_x, bank_x, ring).then_inc(x_scattered[l], 1)

            def step0(i, u, tail=False):
                scatter(0, i, u, 0, ps_agg[0], ps_agg[1])
                at = i * BODY + u if tail else 0
                if at + 1 < TILES:
                    edge_second(i, u + 1)
                if at + 2 < TILES:
                    edge_first(i, u + 2)
                if at + 3 < TILES:
                    attr_transpose(i, u + 3)

            pe.reg_mov(x_done, 0)
            pe.wait_ge(s_control, 1)
            pe.wait_ge(s_b2e3, 16)
            pe.wait_ge(node_out, PAIRS)
            attr_transpose(0, 0)
            edge_first(0, 0)
            attr_transpose(0, 1)
            edge_second(0, 0)
            edge_first(0, 1)
            attr_transpose(0, 2)
            with pe.Fori(0, BODIES - 1) as i:
                for u in range(BODY):
                    step0(i, u)
            for u in range(BODY + 1):
                step0(BODIES - 1, u, tail=True)

            pe.reg_mov(x_done, 0)
            with pe.Fori(0, BODIES) as i:
                for u in range(BODY):
                    scatter(1, i, u, u % 2, ps_agg[u % 2], ps_z[0])
            scatter(1, BODIES, 0, 0, ps_agg[0], ps_z[0])

            pe.wait_ge(all_added, 1)
            for c in range(CHUNKS2):
                if c >= 2:
                    pe.wait_ge(bias_added, c - 1)
                for b in range(CH2):
                    for pr in range(2):
                        last = nc.tensor.matmul(
                            ps_o[c % 2][:, b * F : (b + 1) * F], acc1[:, c * CH2 + b, pr, :], basis[:, pr, :],
                            start=(pr == 0), stop=(pr == 1),
                        )
                last.then_inc(transformed, 1)


_INS = ['x', 'src', 'dst', 'edge_attr_32', 'edge_type_8', 'edge_weight1', 'L0_gnn_W1n', 'L0_gnn_b1n', 'L0_gnn_W2n',
        'L0_gnn_b2n', 'L0_gnn_W1e', 'L0_gnn_b1e', 'L0_gnn_W2e', 'L0_gnn_b2e', 'L0_gnn_res_w', 'L0_gnn_dp_scale',
        'L0_gnn_gamma', 'L0_gnn_beta', 'L1_gnn_weight', 'L1_gnn_w_comp', 'L1_gnn_h_bias']
_OUTS = [((12500, 64), 'float32')]


def kernel(**inputs):
    import numpy as _np
    import concourse.bacc as _bacc
    from concourse import mybir as _mybir
    from concourse.bass_utils import run_bass_kernel_spmd as _run

    nc = _bacc.Bacc("TRN2", target_bir_lowering=False, num_devices=1)
    arrays, args = {}, []
    for name in _INS:
        a = _np.ascontiguousarray(inputs[name])
        arrays[f"in_{name}_dram"] = a
        args.append(nc.dram_tensor(f"in_{name}_dram", a.shape, _mybir.dt.from_np(a.dtype), kind="ExternalInput").ap())
    for i, (shape, dtype) in enumerate(_OUTS):
        dt = _mybir.dt.from_np(_np.dtype(dtype))
        args.append(nc.dram_tensor(f"out_{i}_dram", shape, dt, kind="ExternalOutput").ap())
    bass_gnn_resnorm_d2_kernel(nc, *args)
    r = _run(nc, [arrays], core_ids=[0])
    got = tuple(r.results[0][f"out_{i}_dram"] for i in range(len(_OUTS)))
    return got[0]
```

```python
import concourse.bass as bass
from concourse import mybir
from contextlib import ExitStack


def bass_gnn_resnorm_d2_kernel(
    nc: bass.Bass,
    x: bass.AP,
    src: bass.AP,
    dst: bass.AP,
    edge_attr: bass.AP,
    edge_type: bass.AP,
    edge_weight: bass.AP,
    W1n: bass.AP,
    b1n: bass.AP,
    W2n: bass.AP,
    b2n: bass.AP,
    W1e: bass.AP,
    b1e: bass.AP,
    W2e: bass.AP,
    b2e: bass.AP,
    res_w: bass.AP,
    dp_scale: bass.AP,
    gamma: bass.AP,
    beta: bass.AP,
    rel_basis: bass.AP,
    w_comp: bass.AP,
    h_bias: bass.AP,
    out: bass.AP,
):
    f32 = mybir.dt.float32
    bf16 = mybir.dt.bfloat16
    i32 = mybir.dt.int32
    ALU = mybir.AluOpType
    ACT = mybir.ActivationFunctionType
    AX = mybir.AxisListType

    P = 128
    N, F = x.shape
    E, DE = edge_attr.shape
    R, B = w_comp.shape
    H = W1n.shape[1]
    SLOPE, EPS = 0.1, 1e-5
    assert F == 64 and H == P and DE * 4 == P and B == 4 and 2 * F == P

    NB = -(-N // P)
    LAST_ROWS = N - (NB - 1) * P
    PAIRS = NB // 2
    assert NB == 2 * PAIRS and PAIRS % 2 == 1
    J = 4
    ST = P * J
    FULL = E // ST
    TAIL_P = (E - FULL * ST) // J
    assert TAIL_P * J == E - FULL * ST and 0 < TAIL_P < P
    GROUP = 5
    BODY = 2 * GROUP
    BODIES = FULL // BODY
    assert FULL == BODY * BODIES
    TILES = FULL + 1
    AHEAD = 3

    RC = FULL // P
    R_REST = FULL - RC * P

    node_table = nc.dram_tensor("node_table", (NB * P, F), f32, kind="Internal").ap()
    node_table2 = nc.dram_tensor("node_table2", (NB * P, F), f32, kind="Internal").ap()

    def grouped(a):
        return a[0 : FULL * ST].rearrange("(g s p j) -> g p s j", s=GROUP, p=P, j=J)

    def rest(a):
        return a[FULL * ST : E].rearrange("(p j) -> p j", j=J)

    weight_flat = edge_weight.rearrange("e o -> (e o)")
    attr_groups = edge_attr[0 : FULL * ST, :].rearrange("(g s p j) k -> g p s (j k)", s=GROUP, p=P, j=J)
    attr_rest = edge_attr[FULL * ST : E, :].rearrange("(p j) k -> p (j k)", j=J)

    ctx = ExitStack()
    with ctx:

        def sb(name, shape, dt=f32):
            return ctx.enter_context(nc.sbuf_tensor(name, shape, dt))

        def pb(name, shape, dt=f32):
            return ctx.enter_context(nc.psum_tensor(name, shape, dt))

        def sem(name):
            return ctx.enter_context(nc.semaphore(name))

        x_sb = sb("x_sb", [P, NB, F])
        acc0 = sb("acc0", [P, NB + 1, F])
        acc1 = sb("acc1", [P, 2, (NB + 1) * P])
        work = sb("work", [P, NB * F])
        xt_all = work[:, :].rearrange("p (b f) -> p b f", f=F)
        scaled = work[:, 0 : 2 * J * B * F].rearrange("p (r j b f) -> p r j b f", r=2, j=J, b=B)
        work_i = work[:, :].bitcast(i32)
        at_w = 2 * J * B * F
        is_rel = work[:, at_w : at_w + GROUP * J * R].rearrange("p (e r) -> p e r", r=R)
        at_w += GROUP * J * R
        coef_terms = work[:, at_w : at_w + GROUP * J * B * R].rearrange("p (e b r) -> p e b r", b=B, r=R)
        at_w += GROUP * J * B * R
        onehot_x = work[:, at_w : at_w + J * P].rearrange("p (j n) -> p j n", j=J)
        at_w += J * P
        onehot = work[:, at_w : at_w + 2 * J * P].rearrange("p (r j n) -> p r j n", r=2, j=J)
        dst_rows = work_i[:, 0 : RC * ST].rearrange("p (c e) -> p c e", c=RC)
        dst_rows_r = work_i[0:R_REST, RC * ST : (RC + 1) * ST]
        dst_rows_t = work_i[0:1, (RC + 1) * ST : (RC + 1) * ST + TAIL_P * J]
        at_w = (RC + 2) * ST
        b2e_parts = work[0:1, at_w : at_w + 3 * J * F // 2].bitcast(bf16).rearrange(
            "o (t j f) -> o t j f", t=3, j=J)
        rows = sb("rows", [P, BODY, J, F])
        attr = sb("attr", [P, 2, GROUP, J * DE])
        src_ix = sb("src_ix", [P, 2, GROUP * J], i32)
        dst_ix = sb("dst_ix", [P, 2, GROUP * J], i32)
        GJ = GROUP * J
        attr_flat = attr[:, :, :, :].rearrange("p h s k -> p (h s k)")
        etype = attr_flat[:, 0 : 2 * GJ].bitcast(i32).rearrange("p (h e) -> p h e", h=2)
        enorm = attr_flat[:, 2 * GJ : 4 * GJ].rearrange("p (h e) -> p h e", h=2)
        coef = attr_flat[:, 4 * GJ : (4 + 2 * B) * GJ].rearrange("p (h e b) -> p h e b", h=2, b=B)
        rel = sb("rel", [P, 2, GROUP, J])
        rel_x = sb("rel_x", [P, J])
        x_pair = rows[:, 0, :, :].rearrange("p (k b) f -> p k (b f)", k=2)
        attrT = sb("attrT", [P, P])
        low = sb("low", [P, 2, 2 * P])
        hid = sb("hid", [P, 2, 2 * P])
        msg = work[:, 0 : 2 * J * F].rearrange("p (r j f) -> p r j f", r=2, j=J)

        ident = sb("ident", [P, P])
        iota_i = work_i[:, NB * F - P : NB * F]
        iota_f = sb("iota_f", [P, R])
        W1n_d = sb("W1n_d", [P, 2, H])
        W2n_s = sb("W2n_s", [H, F])
        b1n_c = sb("b1n_c", [H, 1])
        b1n_low = sb("b1n_low", [H, 1])
        b2n_r = sb("b2n_r", [P, F])
        W1e_d = sb("W1e_d", [P, 2, P])
        W2e_d = sb("W2e_d", [P, P])
        b1e_c = sb("b1e_c", [P, 1])
        b1e_low = sb("b1e_low", [P, 1])
        b2e_f = sb("b2e_f", [1, F])
        b2e_res = sb("b2e_res", [1, F])
        b2e_up = sb("b2e_up", [1, F])
        b2e_3 = sb("b2e_3", [3, J * F], bf16)
        ones_3 = sb("ones_3", [3, P], bf16)
        gamma_r = sb("gamma_r", [P, F])
        beta_r = sb("beta_r", [P, F])
        hbias_r = sb("hbias_r", [P, F])
        res_c = sb("res_c", [P, 1])
        dp_c = sb("dp_c", [P, 1])
        scale_c = sb("scale_c", [P, 1])
        basis = sb("basis", [P, 2, F])
        wcomp_r = sb("wcomp_r", [P, R, B])
        RCH = RC + 2
        spans_i = sb("spans_i", [P, RCH, 2], i32)
        spans = sb("spans", [P, RCH, 2])
        base = sb("base", [P, TILES])
        control = sb("control", [1, TILES, 3], i32)
        turn = work[:, 0:TILES]
        turn_i = work_i[:, TILES : 2 * TILES]
        block_i = work_i[0:1, 2 * TILES : 3 * TILES]
        mask_hi = sb("mask_hi", [P, TILES], bf16)
        mask_lo = sb("mask_lo", [P, TILES], bf16)
        part_i = sb("part_i", [P, 1], i32)
        part_f = sb("part_f", [P, 1])
        CH = 14
        CHUNKS = NB // CH
        CH2 = 7
        CHUNKS2 = NB // CH2
        mean = low[:, 0, 0:NB]
        var = low[:, 1, 0:NB]

        ps_T = pb("ps_T", [P, P])
        ps_z = pb("ps_z", [P, 512])
        ps_o = [pb(f"ps_o{k}", [P, 512]) for k in range(2)]
        ps_agg = [pb(f"ps_agg{k}", [P, 512]) for k in range(2)]
        ps_x = pb("ps_x", [P, 512])
        ps_iota = pb("ps_iota", [P, 512])
        node_z = [ps_z, ps_x]

        s_const = sem("s_const")
        s_x = sem("s_x")
        s_rows = sem("s_rows")
        s_pool = sem("s_pool")
        s_zero = sem("s_zero")
        s_b2e = sem("s_b2e")
        s_b2e3 = sem("s_b2e3")
        s_setup = sem("s_setup")
        s_spans = sem("s_spans")
        s_bcast = sem("s_bcast")
        s_control = sem("s_control")
        s_dve = sem("s_dve")
        node_staged = sem("node_staged")
        node_T = sem("node_T")
        node_copied = sem("node_copied")
        node_mm1 = sem("node_mm1")
        node_low = sem("node_low")
        node_hid = sem("node_hid")
        node_mm2 = sem("node_mm2")
        node_out = sem("node_out")
        table_ready = sem("table_ready")
        table2_ready = sem("table2_ready")
        s_out = sem("s_out")

        attr_loaded = [sem(f"attr_loaded{h}") for h in range(2)]
        src_loaded = [[sem(f"src_loaded{l}{h}") for h in range(2)] for l in range(2)]
        dst_loaded = [[sem(f"dst_loaded{l}{h}") for h in range(2)] for l in range(2)]
        type_loaded = [sem(f"type_loaded{h}") for h in range(2)]
        norm_loaded = [sem(f"norm_loaded{h}") for h in range(2)]
        gathered = [[sem(f"gathered{l}_{u}") for u in range(BODY)] for l in range(2)]
        transposed = sem("transposed")
        attr_copied = sem("attr_copied")
        mm1_done = sem("mm1_done")
        low_ready = sem("low_ready")
        hid_ready = sem("hid_ready")
        mm2_done = sem("mm2_done")
        msg_ready = [sem("msg_ready"), sem("scaled_ready")]
        rel_ready = [sem(f"rel_ready{l}") for l in range(2)]
        rel_moved = [sem(f"rel_moved{l}") for l in range(2)]
        s_link = sem("s_link")
        gathers_begun = sem("gathers_begun")
        all_added = sem("all_added")
        scattered = [sem(f"scattered{l}") for l in range(2)]
        added = [sem(f"added{l}") for l in range(2)]
        x_onehot_ready = [sem(f"x_onehot_ready{l}") for l in range(2)]
        x_scattered = [sem(f"x_scattered{l}") for l in range(2)]
        x_added = [sem(f"x_added{l}") for l in range(2)]
        centered = sem("centered")
        squared = sem("squared")
        var_ready = sem("var_ready")
        std_ready = sem("std_ready")
        normed = sem("normed")
        transformed = sem("transformed")
        bias_added = sem("bias_added")
        normed2 = sem("normed2")

        block = ctx.enter_context(nc.Block())

        def tile_of(i, u):
            return i * BODY + u

        def slot_of(u):
            return u % BODY

        def half_of(u):
            return (u % BODY) // GROUP

        def uses(i, u):
            return i + (u // BODY) + 1

        def const_loads(sp):
            n = 0

            def ld(o, i):
                nonlocal n
                sp.dma_start(o, i).then_inc(s_const, 16)
                n += 1

            ld(W1n_d[0:F, 0, :], W1n)
            ld(W1n_d[F:P, 1, :], W1n)
            ld(W2n_s[:], W2n)
            ld(b1n_c[:], b1n.rearrange("(p o) -> p o", o=1))
            ld(b2n_r[:], b2n.rearrange("(o f) -> o f", o=1).to_broadcast([P, F]))
            for pr in range(2):
                for h in range(2):
                    at = (2 * pr + h) * DE
                    ld(W1e_d[at : at + DE, pr, h * F : h * F + F], W1e)
            ld(W2e_d[0:F, 0:F], W2e)
            ld(W2e_d[F:P, F:P], W2e)
            b1e_v = b1e.rearrange("(p o) -> p o", o=1)
            ld(b1e_c[0:F, :], b1e_v)
            ld(b1e_c[F:P, :], b1e_v)
            ld(b2e_f[:], b2e.rearrange("(o f) -> o f", o=1))
            ld(gamma_r[:], gamma.rearrange("(o f) -> o f", o=1).to_broadcast([P, F]))
            ld(beta_r[:], beta.rearrange("(o f) -> o f", o=1).to_broadcast([P, F]))
            ld(hbias_r[:], h_bias.rearrange("(o f) -> o f", o=1).to_broadcast([P, F]))
            ld(res_c[:], res_w.rearrange("(o f) -> o f", o=1).to_broadcast([P, 1]))
            ld(dp_c[:], dp_scale.rearrange("(o f) -> o f", o=1).to_broadcast([P, 1]))
            ld(basis[:], rel_basis.rearrange("(q b) i o -> (b i) q o", q=2))
            ld(
                wcomp_r[:].rearrange("p r b -> p (r b)"),
                w_comp.rearrange("(o r) b -> o (r b)", o=1).to_broadcast([P, R * B]),
            )
            return n

        CONST_LOADS = 21
        NODE_STORES = PAIRS // 2 + 1
        MID_STORES = CHUNKS
        ALL_GATHERS = 16 * J

        @block.sync
        def _(sp):
            x_main = x[0 : (NB - 1) * P, :].rearrange("(b p) f -> p b f", p=P)
            cut = 16
            sp.dma_start(x_sb[:, 0:cut, :], x_main[:, 0:cut, :]).then_inc(s_x, 16)
            sp.wait_ge(s_zero, 4)
            n = const_loads(sp)
            assert n == CONST_LOADS, n
            sp.dma_start(x_sb[:, cut : NB - 1, :], x_main[:, cut:, :]).then_inc(s_rows, 16)
            sp.dma_start(x_sb[0:LAST_ROWS, NB - 1, :], x[(NB - 1) * P : N, :]).then_inc(s_rows, 16)
            sp.dma_start(
                dst_rows, dst[0 : RC * P * ST].rearrange("(c p e) -> p c e", c=RC, p=P)
            ).then_inc(s_rows, 16)
            sp.dma_start(
                dst_rows_r, dst[RC * P * ST : FULL * ST].rearrange("(p e) -> p e", e=ST)
            ).then_inc(s_rows, 16)
            sp.dma_start(
                dst_rows_t, dst[FULL * ST : E].rearrange("(o e) -> o e", o=1)
            ).then_inc(s_rows, 16)
            sp.wait_ge(s_b2e, 1)
            sp.dma_start(b2e_3[:], b2e_parts.rearrange("o t j f -> o t (j f)")).then_inc(s_b2e3, 16)

            def load_group(l, h, g):
                sp.dma_start(
                    src_ix[:, h, :].rearrange("p (s j) -> p s j", j=J), grouped(src)[g]
                ).then_inc(src_loaded[l][h], 16)
                sp.dma_start(
                    dst_ix[:, h, :].rearrange("p (s j) -> p s j", j=J), grouped(dst)[g]
                ).then_inc(dst_loaded[l][h], 16)
                if l == 0:
                    sp.dma_start(attr[:, h, :, :], attr_groups[g]).then_inc(attr_loaded[h], 16)
                else:
                    sp.dma_start(
                        etype[:, h, :].rearrange("p (s j) -> p s j", j=J), grouped(edge_type)[g]
                    ).then_inc(type_loaded[h], 16)
                    sp.dma_start(
                        enorm[:, h, :].rearrange("p (s j) -> p s j", j=J), grouped(weight_flat)[g]
                    ).then_inc(norm_loaded[h], 16)

            def load_tail(l):
                sp.dma_start(src_ix[0:TAIL_P, 0, 0:J], rest(src)).then_inc(src_loaded[l][0], 16)
                sp.dma_start(dst_ix[0:TAIL_P, 0, 0:J], rest(dst)).then_inc(dst_loaded[l][0], 16)
                if l == 0:
                    sp.dma_start(attr[0:TAIL_P, 0, 0, :], attr_rest).then_inc(attr_loaded[0], 16)
                else:
                    sp.dma_start(etype[0:TAIL_P, 0, 0:J], rest(edge_type)).then_inc(type_loaded[0], 16)
                    sp.dma_start(enorm[0:TAIL_P, 0, 0:J], rest(weight_flat)).then_inc(norm_loaded[0], 16)

            def layer_loads(l):
                with sp.Fori(0, BODIES - 1) as i:
                    for h in range(2):
                        sp.wait_ge(msg_ready[l], i * BODY + (h + 1) * GROUP)
                        load_group(l, h, i * 2 + (2 + h))
                sp.wait_ge(msg_ready[l], (BODIES - 1) * BODY + GROUP)
                load_tail(l)

            for h in range(2):
                load_group(0, h, h)
            table_v = node_table[0 : (NB - 2) * P, :].rearrange("(i b p) f -> i p b f", b=4, p=P)
            with sp.Fori(0, PAIRS // 2) as i:
                sp.wait_ge(node_out, i * 2 + 2)
                sp.dma_start(table_v[i], xt_all[:, bass.ds(i * 4, 4), :]).then_inc(table_ready, 16)
            sp.wait_ge(node_out, PAIRS)
            sp.dma_start(
                node_table[(NB - 2) * P :, :].rearrange("(b p) f -> p b f", p=P), xt_all[:, NB - 2 :, :]
            ).then_inc(table_ready, 16)
            layer_loads(0)
            sp.wait_ge(msg_ready[0], TILES)
            for h in range(2):
                load_group(1, h, h)
            for c in range(CHUNKS):
                sp.wait_ge(normed, c + 1)
                sp.dma_start(
                    node_table2[c * CH * P : (c + 1) * CH * P, :].rearrange("(b p) f -> p b f", p=P),
                    x_sb[:, c * CH : (c + 1) * CH, :],
                ).then_inc(table2_ready, 16)
            layer_loads(1)
            for c in range(CHUNKS2):
                sp.wait_ge(normed2, c + 1)
                lo, hi = c * CH2, min((c + 1) * CH2, NB - 1)
                sp.dma_start(
                    out[lo * P : hi * P, :].rearrange("(b p) f -> p b f", p=P), x_sb[:, lo:hi, :]
                ).then_inc(s_out, 16)
            sp.dma_start(out[(NB - 1) * P : N, :], x_sb[0:LAST_ROWS, NB - 1, :]).then_inc(s_out, 16)
            sp.wait_ge(s_out, 16 * (CHUNKS2 + 1))

        @block.gpsimd
        def _(pool):
            nc.gpsimd.memset(W1n_d[:], 0.0).then_inc(s_zero, 1)
            nc.gpsimd.memset(W1e_d[:], 0.0).then_inc(s_zero, 1)
            nc.gpsimd.memset(W2e_d[:], 0.0).then_inc(s_zero, 1)
            nc.gpsimd.memset(x_sb[:, NB - 1, :], 0.0).then_inc(s_zero, 1)
            nc.gpsimd.memset(ident[:], 0.0).then_inc(s_pool, 1)
            nc.gpsimd.iota(iota_i, pattern=[[1, P]], base=0, channel_multiplier=0).then_inc(s_pool, 1)
            nc.gpsimd.iota(part_i[:], pattern=[[0, 1]], base=0, channel_multiplier=1).then_inc(s_pool, 1)
            pool.wait_ge(s_pool, 3)
            nc.gpsimd.affine_select(
                out=ident[:], in_=ident[:], compare_op=ALU.not_equal, fill=1.0, base=0,
                pattern=[[-1, P]], channel_multiplier=1,
            ).then_inc(s_pool, 1)
            nc.gpsimd.memset(ones_3[:], 1.0).then_inc(s_pool, 1)

            def stage(q, k):
                pool.wait_ge(s_rows, 16 * 5)
                nc.gpsimd.tensor_copy(
                    x_pair[:, k, :], x_sb[:, bass.ds(q * 2, 2), :].rearrange("p b f -> p (b f)")
                ).then_inc(node_staged, 1)

            pool.wait_ge(s_x, 16)
            for q in range(3):
                if q == 2:
                    pool.wait_ge(node_T, 1)
                stage(q, q % 2)
            with pool.Fori(1, PAIRS // 2) as i:
                for k in range(2):
                    pool.wait_ge(node_T, i * 2 + k)
                    stage(i * 2 + (k + 1), 1 - k)
            nc.gpsimd.memset(acc0[:], 0.0).then_inc(s_pool, 1)
            nc.gpsimd.memset(acc1[:], 0.0).then_inc(s_pool, 1)

            def gather(l, i, u, slot_used=None):
                table = (node_table, node_table2)[l]
                if slot_used is not None:
                    pool.wait_ge(msg_ready[l], slot_used)
                if (u % GROUP) == 0:
                    pool.wait_ge(src_loaded[l][half_of(u)], uses(i, u) * 16)
                pool.sem_inc(gathers_begun, 1)
                for j in range(J):
                    col = (u % GROUP) * J + j
                    nc.gpsimd.indirect_dma_start(
                        rows[:, slot_of(u), j, :], None, table,
                        bass.IndirectOffsetOnAxis(ap=src_ix[:, half_of(u), col : col + 1], axis=0),
                    ).then_inc(gathered[l][slot_of(u)], 16)

            for l in range(2):
                ready, count = ((table_ready, 16 * NODE_STORES), (table2_ready, 16 * MID_STORES))[l]
                pool.wait_ge(ready, count)
                for u in range(BODY):
                    gather(l, 0, u)
                with pool.Fori(1, BODIES) as i:
                    for u in range(BODY):
                        gather(l, i, u, i * BODY + (u + 1 - BODY))
                gather(l, BODIES, 0, FULL + 1 - BODY)

        @block.scalar
        def _(act):
            act.wait_ge(s_const, 16 * CONST_LOADS)
            nc.scalar.mul(b1n_low[:], b1n_c[:], SLOPE).then_inc(s_setup, 1)
            nc.scalar.mul(b1e_low[:], b1e_c[:], SLOPE).then_inc(s_setup, 1)
            act.wait_ge(s_setup, 2)

            def node_copy(q):
                act.wait_ge(node_T, q + 1)
                nc.scalar.copy(attrT[:], ps_T[:]).then_inc(node_copied, 1)

            def node_lower(q, k):
                act.wait_ge(node_mm1, q + 1)
                nc.scalar.activation(
                    low[:, k, :], node_z[k][:, 0 : 2 * P], ACT.Identity, bias=b1n_low[:], scale=SLOPE
                ).then_inc(node_low, 1)

            node_copy(0)
            with act.Fori(0, PAIRS // 2) as i:
                for k in range(2):
                    node_copy(i * 2 + (k + 1))
                    node_lower(i * 2 + k, k)
            node_lower(PAIRS - 1, 0)

            def edge_copy(i, u):
                act.wait_ge(transposed, tile_of(i, u) + 1)
                nc.scalar.copy(attrT[:], ps_T[:]).then_inc(attr_copied, 1)

            def edge_lower(i, u):
                act.wait_ge(mm1_done, tile_of(i, u) + 1)
                nc.scalar.activation(
                    low[:, 0, :], ps_z[:, 0 : 2 * P], ACT.Identity, bias=b1e_low[:], scale=SLOPE
                ).then_inc(low_ready, 1)

            def step(i, u, last=TILES):
                if last is None or i * BODY + u + 2 < TILES:
                    edge_lower(i, u + 2)
                if last is None or i * BODY + u + 3 < TILES:
                    edge_copy(i, u + 3)

            edge_copy(0, 0)
            edge_lower(0, 0)
            edge_copy(0, 1)
            edge_lower(0, 1)
            edge_copy(0, 2)
            with act.Fori(0, BODIES - 1) as i:
                for u in range(BODY):
                    step(i, u, None)
            for u in range(BODY + 1):
                step(BODIES - 1, u)

            def square(k, count, cols):
                act.wait_ge(centered, count)
                nc.scalar.activation(work[:, cols], acc0[:, :, :].rearrange("p b f -> p (b f)")[:, cols],
                                     ACT.Square).then_inc(squared, 1)

            def root(count, blocks):
                act.wait_ge(var_ready, count)
                nc.scalar.activation(var[:, blocks], var[:, blocks], ACT.Sqrt).then_inc(std_ready, 1)

            def chunk(c, n):
                return slice(c * n * F, (c + 1) * n * F), slice(c * n, (c + 1) * n)

            n = 0
            for c in range(CHUNKS):
                for norm in range(2):
                    n += 1
                    cols, blocks = chunk(c, CH)
                    square(0, n, cols)
                    root(n, blocks)
            for c in range(CHUNKS2):
                n += 1
                cols, blocks = chunk(c, CH2)
                square(0, n, cols)
                root(n, blocks)

        @block.vector
        def _(dve):
            steps = [0]

            def link(ins):
                steps[0] += 1
                ins.then_inc(s_dve, 1)
                dve.wait_ge(s_dve, steps[0])

            dve.wait_ge(s_pool, 3)
            for k in range(2):
                nc.vector.tensor_copy(ps_iota[:, k * P : (k + 1) * P], iota_i)
            nc.vector.tensor_copy(part_f[:], part_i[:])
            nc.vector.tensor_copy(iota_f[:], iota_i[:, 0:R])
            link(nc.vector.memset(spans_i[:], 0))
            dve.wait_ge(s_const, 16 * CONST_LOADS)
            link(nc.vector.tensor_tensor(scale_c[:], res_c[:], dp_c[:], ALU.mult))
            rest_of = b2e_f
            for t in range(3):
                part = b2e_parts[:, t, :, :]
                link(nc.vector.tensor_copy(part, rest_of[:].rearrange("o (j f) -> o j f", j=1).to_broadcast([1, J, F])))
                if t < 2:
                    link(nc.vector.tensor_copy(b2e_up[:], b2e_parts[:, t, 0, :]))
                    link(nc.vector.tensor_tensor(b2e_res[:], rest_of[:], b2e_up[:], ALU.subtract))
                    rest_of = b2e_res
            dve.sem_inc(s_b2e, 1)

            dve.wait_ge(s_rows, 16 * 5)
            for v, op in enumerate((ALU.min, ALU.max)):
                nc.vector.tensor_reduce(spans_i[:, 0:RC, v], dst_rows, axis=AX.X, op=op)
                nc.vector.tensor_reduce(spans_i[0:R_REST, RC, v : v + 1], dst_rows_r, axis=AX.X, op=op)
                link(nc.vector.tensor_reduce(spans_i[0:1, RC + 1, v : v + 1], dst_rows_t, axis=AX.X, op=op))
            link(nc.vector.tensor_copy(spans[:], spans_i[:]))
            link(nc.vector.tensor_tensor(spans_i[:, :, 1], spans[:, :, 1], spans[:, :, 0], ALU.subtract))
            link(nc.vector.tensor_scalar(spans_i[:, :, 1], spans_i[:, :, 1], 7, None, ALU.logical_shift_right))
            nc.vector.tensor_copy(spans[:, :, 1], spans_i[:, :, 1]).then_inc(s_spans, 1)
            dve.wait_ge(s_bcast, 1)
            nc.vector.tensor_copy(base[:], ps_agg[0][:, 0:TILES])
            nc.vector.tensor_copy(control[:, :, 0], ps_agg[1][0:1, 0:TILES])
            link(nc.vector.tensor_copy(turn_i, ps_agg[0][:, 0:TILES]))
            link(nc.vector.tensor_scalar(block_i, turn_i[0:1, :], 7, None, ALU.logical_shift_right))
            link(nc.vector.tensor_scalar(turn_i, turn_i, P - 1, None, ALU.bitwise_and))
            link(nc.vector.tensor_copy(turn, turn_i))
            nc.vector.tensor_copy(control[:, :, 2], block_i)
            link(nc.vector.tensor_scalar(control[:, :, 1], turn[0:1, :], -1.0, float(P), ALU.mult, ALU.add))
            dve.sem_inc(s_control, 1)
            nc.vector.tensor_scalar(mask_hi[:], turn, part_f[:], None, ALU.is_le)
            link(nc.vector.tensor_scalar(mask_lo[:], turn, part_f[:], None, ALU.is_gt))

            def node_hidden(q, k):
                dve.wait_ge(node_low, q + 1)
                nc.vector.scalar_tensor_tensor(
                    hid[:, k, :], node_z[k][:, 0 : 2 * P], b1n_c[:], low[:, k, :], ALU.add, ALU.max
                ).then_inc(node_hid, 1)

            def node_store(q, k):
                dve.wait_ge(node_mm2, q + 1)
                nc.vector.tensor_tensor(
                    xt_all[:, bass.ds(q * 2, 2), :],
                    ps_o[k][:, 0 : 2 * F].rearrange("p (b f) -> p b f", b=2),
                    b2n_r[:].rearrange("p (o f) -> p o f", o=1).to_broadcast([P, 2, F]),
                    ALU.add,
                ).then_inc(node_out, 1)

            dve.wait_ge(s_b2e3, 16)
            node_hidden(0, 0)
            with dve.Fori(0, PAIRS // 2) as i:
                for k in range(2):
                    node_hidden(i * 2 + (k + 1), 1 - k)
                    node_store(i * 2 + k, k)
            node_store(PAIRS - 1, 0)

            window, further, rotation, first_block = (
                [dve.alloc_register(f"dve_{name}{n}") for n in range(2)]
                for name in ("window", "further", "rotation", "first_block")
            )
            k_reg, x_done = (dve.alloc_register(f"dve_{n}") for n in ("k", "x_done"))

            def span_of(l, i, u):
                ring = u % 2
                regs, cols = (
                    ([further[ring], rotation[ring], first_block[ring]], slice(0, 3)),
                    ([further[ring], window[ring]], slice(0, 2)),
                )[l]
                dve.reg_load(regs, control[0:1, bass.ds(tile_of(i, u), 1), cols].rearrange("p o v -> p (o v)"))

            def relative(l, i, u):
                h = half_of(u)
                dve.wait_ge(dst_loaded[l][h], uses(i, u) * 16)
                s = tile_of(i, u)
                nc.vector.tensor_tensor(
                    rel[:, h, :, :],
                    dst_ix[:, h, :].rearrange("p (s j) -> p s j", j=J),
                    base[:, bass.ds(s, GROUP)].rearrange("p (s o) -> p s o", o=1).to_broadcast([P, GROUP, J]),
                    ALU.subtract,
                ).then_inc(rel_ready[l], 1)
                dve.wait_ge(rel_ready[l], i * 2 + (u // GROUP) + 1)

            def relative_tail(l):
                dve.wait_ge(dst_loaded[l][0], (BODIES + 1) * 16)
                nc.vector.memset(rel[:, 0, 0, :], -1.0).then_inc(rel_ready[l], 1)
                dve.wait_ge(rel_ready[l], BODIES * 2 + 1)
                nc.vector.tensor_tensor(
                    rel[0:TAIL_P, 0, 0, :],
                    dst_ix[0:TAIL_P, 0, 0:J],
                    base[0:TAIL_P, FULL : FULL + 1].to_broadcast([TAIL_P, J]),
                    ALU.subtract,
                ).then_inc(rel_ready[l], 1)
                dve.wait_ge(rel_ready[l], BODIES * 2 + 2)

            def one_hot(l, o, r, ring):
                at = bass.ds(dve.snap(rotation[ring]), P) if l == 0 else slice(0, P)
                return nc.vector.tensor_tensor(
                    o,
                    ps_iota[:, at].rearrange("p (o n) -> p o n", o=1).to_broadcast([P, J, P]),
                    r.rearrange("p (j o) -> p j o", o=1).to_broadcast([P, J, P]),
                    ALU.is_equal,
                )

            def add_window(l, s, ring, k, bank):
                if l == 1:
                    w = dve.snap(window[ring])
                    a = acc1[:, :, bass.ds(w + k * P, P)]
                    return nc.vector.tensor_tensor(
                        a, a, bank[:, 0 : 2 * P].rearrange("p (q n) -> p q n", q=2), ALU.add)
                first = dve.snap(first_block[ring])
                for b, mask in enumerate((mask_hi, mask_lo)):
                    a = acc0[:, bass.ds(first + k + b, 1), :].rearrange("p o f -> p (o f)")
                    last = nc.vector.scalar_tensor_tensor(
                        a, bank[:, 0:F], mask[:, bass.ds(s, 1)], a, ALU.mult, ALU.add)
                return last

            def add_sums(l, i, u, bank, last=False):
                if last:
                    dve.wait_ge(added[l], FULL + 1)
                dve.wait_ge(scattered[l], tile_of(i, u) + 1)
                add_window(l, tile_of(i, u), u % 2, 0, bank).then_inc(added[l], 1)

            def extras(l, i, u):
                s = tile_of(i, u)
                dve.reg_mov(k_reg, 0)
                with dve.While(lambda: dve.snap(k_reg) < dve.snap(further[u % 2])):
                    r = rel[:, half_of(u), u % GROUP, :]
                    dve.wait_ge(added[l], s + 2)
                    dve.reg_add(x_done, x_done, 1)
                    nc.vector.tensor_scalar(r, r, float(P), None, ALU.subtract).then_inc(rel_moved[l], 1)
                    dve.wait_ge(rel_moved[l], dve.snap(x_done))
                    one_hot(l, onehot_x, r, u % 2).then_inc(x_onehot_ready[l], 1)
                    dve.wait_ge(x_scattered[l], dve.snap(x_done))
                    add_window(l, s, u % 2, dve.snap(k_reg) + 1, ps_x).then_inc(x_added[l], 1)
                    dve.wait_ge(x_added[l], dve.snap(x_done))
                    dve.reg_add(k_reg, k_reg, 1)

            def main_one_hot(l, i, u):
                if u > 0 or not (isinstance(i, int) and i == 0):
                    dve.wait_ge(added[l], tile_of(i, u))
                one_hot(l, onehot[:, u % 2, :, :], rel[:, half_of(u), u % GROUP, :], u % 2)

            def edge_hidden(i, u):
                dve.wait_ge(low_ready, tile_of(i, u) + 1)
                nc.vector.scalar_tensor_tensor(
                    hid[:, 0, :], ps_z[:, 0 : 2 * P], b1e_c[:], low[:, 0, :], ALU.add, ALU.max
                ).then_inc(hid_ready, 1)

            def message(i, u):
                dve.wait_ge(gathered[0][slot_of(u)], uses(i, u) * ALL_GATHERS)
                dve.wait_ge(mm2_done, tile_of(i, u) + 1)
                nc.vector.tensor_tensor(
                    msg[:, u % 2, :, :].rearrange("p j f -> p (j f)"),
                    ps_o[u % 2][:, 0 : J * F],
                    rows[:, slot_of(u), :, :].rearrange("p j f -> p (j f)"),
                    ALU.mult,
                ).then_inc(msg_ready[0], 1)

            def prepare0(i, u, tail=False):
                span_of(0, i, u)
                if tail:
                    relative_tail(0)
                elif u % GROUP == 0:
                    relative(0, i, u)
                main_one_hot(0, i, u)
                message(i, u)

            def step0(i, u, last=None):
                if last is None or u + 1 <= last:
                    prepare0(i, u + 1, tail=(last is not None and u + 1 == last))
                if last is None or u + 2 <= last:
                    edge_hidden(i, u + 2)
                add_sums(0, i, u, ps_agg[u % 2], last is not None and u == last)
                extras(0, i, u)

            dve.wait_ge(s_pool, 7)
            dve.wait_ge(table_ready, 16 * NODE_STORES)
            for l in range(2):
                dve.sem_inc(added[l], 1)
            dve.reg_mov(x_done, 0)
            edge_hidden(0, 0)
            edge_hidden(0, 1)
            prepare0(0, 0)
            with dve.Fori(0, BODIES - 1) as i:
                for u in range(BODY):
                    step0(i, u)
            for u in range(BODY + 1):
                step0(BODIES - 1, u, last=BODY)

            o_all = acc0[:, :, :].rearrange("p b f -> p (b f)")
            x_all = x_sb[:, :, :].rearrange("p b f -> p (b f)")

            def blocks_of(c, n):
                return slice(c * n * F, (c + 1) * n * F), slice(c * n, (c + 1) * n)

            def by_block(ap, n):
                return ap.rearrange("p (b f) -> p b f", f=F)

            def over_features(ap, n):
                return ap.rearrange("p (b o) -> p b o", o=1).to_broadcast([P, n, F])

            def over_blocks(ap, n):
                return ap.rearrange("p (o f) -> p o f", o=1).to_broadcast([P, n, F])

            def center(c, n):
                cols, bl = blocks_of(c, n)
                o = by_block(o_all[:, cols], n)
                link(nc.vector.tensor_reduce(mean[:, bl], o, axis=AX.X, op=ALU.add))
                link(nc.vector.tensor_scalar(mean[:, bl], mean[:, bl], 1.0 / F, None, ALU.mult))
                nc.vector.tensor_tensor(o, o, over_features(mean[:, bl], n), ALU.subtract).then_inc(centered, 1)

            def variance(c, n, count):
                cols, bl = blocks_of(c, n)
                dve.wait_ge(squared, count)
                link(nc.vector.tensor_reduce(var[:, bl], by_block(work[:, cols], n), axis=AX.X, op=ALU.add))
                nc.vector.tensor_scalar(var[:, bl], var[:, bl], 1.0 / F, EPS, ALU.mult, ALU.add).then_inc(
                    var_ready, 1
                )

            def by_std(o, c, n, count, target):
                cols, bl = blocks_of(c, n)
                dve.wait_ge(std_ready, count)
                link(nc.vector.reciprocal(var[:, bl], var[:, bl]))
                return nc.vector.tensor_tensor(target, o, over_features(var[:, bl], n), ALU.mult)

            n_norm = 0
            for c in range(CHUNKS):
                cols, bl = blocks_of(c, CH)
                o = by_block(o_all[:, cols], CH)
                if c == 0:
                    dve.wait_ge(added[0], TILES + 1)
                link(nc.vector.scalar_tensor_tensor(
                    o_all[:, cols], o_all[:, cols], scale_c[:], x_all[:, cols], ALU.mult, ALU.add))
                center(c, CH)
                n_norm += 1
                variance(c, CH, n_norm)
                link(by_std(o, c, CH, n_norm, o))
                link(nc.vector.tensor_tensor(o, o, over_blocks(gamma_r[:], CH), ALU.mult))
                link(nc.vector.tensor_tensor(o, o, over_blocks(beta_r[:], CH), ALU.add))
                link(nc.vector.tensor_tensor(o_all[:, cols], o_all[:, cols], x_all[:, cols], ALU.add))
                center(c, CH)
                n_norm += 1
                variance(c, CH, n_norm)
                by_std(o, c, CH, n_norm, by_block(x_all[:, cols], CH)).then_inc(normed, 1)

            def coefficients(i, u, rows_p=P, cols=GROUP * J):
                h = half_of(u)
                dve.wait_ge(type_loaded[h], uses(i, u) * 16)
                link_l(nc.vector.tensor_tensor(
                    is_rel,
                    etype[:, h, :].rearrange("p (e o) -> p e o", o=1).to_broadcast([P, GROUP * J, R]),
                    iota_f[:].rearrange("p (o r) -> p o r", o=1).to_broadcast([P, GROUP * J, R]),
                    ALU.is_equal))
                dve.wait_ge(norm_loaded[h], uses(i, u) * 16)
                link_l(nc.vector.tensor_tensor(
                    is_rel, is_rel,
                    enorm[:, h, :].rearrange("p (e o) -> p e o", o=1).to_broadcast([P, GROUP * J, R]),
                    ALU.mult))
                link_l(nc.vector.tensor_tensor(
                    coef_terms,
                    is_rel.rearrange("p e (o r) -> p e o r", o=1).to_broadcast([P, GROUP * J, B, R]),
                    wcomp_r[:].rearrange("p r b -> p b r").rearrange("p (o b) r -> p o b r", o=1).to_broadcast([P, GROUP * J, B, R]),
                    ALU.mult))
                link_l(nc.vector.tensor_reduce(coef[:, h, :, :], coef_terms, axis=AX.X, op=ALU.add))

            l_steps = dve.alloc_register("dve_link")
            dve.reg_mov(l_steps, 0)

            def link_l(ins):
                ins.then_inc(s_link, 1)
                dve.reg_add(l_steps, l_steps, 1)
                dve.wait_ge(s_link, dve.snap(l_steps))

            def scale_rows(i, u, ring):
                dve.wait_ge(gathered[1][slot_of(u)], uses(i, u) * ALL_GATHERS)
                h, at = half_of(u), (u % GROUP) * J
                nc.vector.tensor_tensor(
                    scaled[:, ring, :, :, :],
                    rows[:, slot_of(u), :, :].rearrange("p j (o f) -> p j o f", o=1).to_broadcast([P, J, B, F]),
                    coef[:, h, at : at + J, :].rearrange("p j (b o) -> p j b o", o=1).to_broadcast([P, J, B, F]),
                    ALU.mult,
                ).then_inc(msg_ready[1], 1)

            def prepare1(i, u, tail=False):
                if tail:
                    relative_tail(1)
                    coefficients(i, u)
                elif u % GROUP == 0:
                    relative(1, i, u)
                    coefficients(i, u)
                main_one_hot(1, i, u)
                scale_rows(i, u, u % 2)

            def finish1(i, u, last=False):
                add_sums(1, i, u, ps_agg[u % 2], last)
                extras(1, i, u)

            link(nc.vector.tensor_copy(control[:, :, 1], base[0:1, :]))
            dve.reg_mov(x_done, 0)
            prepare1(0, 0)
            with dve.Fori(0, BODIES - 1) as i:
                for u in range(BODY):
                    span_of(1, i, u)
                    prepare1(i, u + 1)
                    finish1(i, u)
            for u in range(BODY + 1):
                span_of(1, BODIES - 1, u)
                if u < BODY:
                    prepare1(BODIES - 1, u + 1, tail=(u + 1 == BODY))
                finish1(BODIES - 1, u, u == BODY)
            dve.wait_ge(added[1], TILES + 1)
            nc.vector.memset(spans_i[0:1, 0, :], 0).then_inc(all_added, 1)

            for c in range(CHUNKS2):
                cols, bl = blocks_of(c, CH2)
                o = by_block(o_all[:, cols], CH2)
                dve.wait_ge(transformed, c + 1)
                nc.vector.tensor_tensor(
                    o, by_block(ps_o[c % 2][:, 0 : CH2 * F], CH2), over_blocks(hbias_r[:], CH2), ALU.add
                ).then_inc(bias_added, 1)
                dve.wait_ge(bias_added, c + 1)
                link(nc.vector.scalar_tensor_tensor(
                    o_all[:, cols], o_all[:, cols], 0.0, x_all[:, cols], ALU.max, ALU.add))
                center(c, CH2)
                n_norm += 1
                variance(c, CH2, n_norm)
                by_std(o, c, CH2, n_norm, by_block(x_all[:, cols], CH2)).then_inc(normed2, 1)

        @block.tensor
        def _(pe):
            pe.wait_ge(s_pool, 5)
            pe.wait_ge(s_spans, 1)
            for v in range(2):
                for c in range(RCH):
                    rows_c = (P, R_REST, 1)[max(0, c - RC + 1)]
                    at = FULL if c == RCH - 1 else c * P
                    last = nc.tensor.matmul(
                        ps_agg[v][:, at : at + rows_c],
                        spans[0:rows_c, c, v : v + 1].to_broadcast([rows_c, P]),
                        ident[0:rows_c, 0:rows_c], start=True, stop=True,
                    )
            last.then_inc(s_bcast, 1)

            def node_transpose(q, k):
                pe.wait_ge(node_staged, q + 1)
                nc.tensor.transpose(ps_T[:], x_pair[:, k, :], ident[:]).then_inc(node_T, 1)

            def node_first(q, k):
                pe.wait_ge(node_copied, q + 1)
                for b in range(2):
                    last = nc.tensor.matmul(
                        node_z[k][:, b * P : (b + 1) * P], W1n_d[:, b, :], attrT[:], start=True, stop=True
                    )
                last.then_inc(node_mm1, 1)

            def node_second(q, k):
                pe.wait_ge(node_hid, q + 1)
                for b in range(2):
                    last = nc.tensor.matmul(
                        ps_o[k][:, b * F : (b + 1) * F], hid[:, k, b * P : (b + 1) * P], W2n_s[:],
                        start=True, stop=True,
                    )
                last.then_inc(node_mm2, 1)

            pe.wait_ge(s_const, 16 * CONST_LOADS)
            pe.wait_ge(s_x, 16)
            node_transpose(0, 0)
            node_first(0, 0)
            node_transpose(1, 1)
            with pe.Fori(0, PAIRS // 2 - 1) as i:
                for k in range(2):
                    node_first(i * 2 + (k + 1), 1 - k)
                    node_transpose(i * 2 + (k + 2), k)
                    node_second(i * 2 + k, k)
            node_first(PAIRS - 2, 1)
            node_transpose(PAIRS - 1, 0)
            node_second(PAIRS - 3, 0)
            node_first(PAIRS - 1, 0)
            node_second(PAIRS - 2, 1)
            node_second(PAIRS - 1, 0)

            further, k_reg, x_done = (pe.alloc_register(f"pe_{n}") for n in ("further", "k", "x_done"))

            def attr_transpose(i, u):
                if u % GROUP == 0:
                    pe.wait_ge(attr_loaded[half_of(u)], uses(i, u) * 16)
                nc.tensor.transpose(ps_T[:], attr[:, half_of(u), u % GROUP, :], ident[:]).then_inc(
                    transposed, 1
                )

            def edge_first(i, u):
                pe.wait_ge(attr_copied, tile_of(i, u) + 1)
                for pr in range(2):
                    last = nc.tensor.matmul(
                        ps_z[:, pr * P : (pr + 1) * P], W1e_d[:, pr, :], attrT[:], start=True, stop=True
                    )
                last.then_inc(mm1_done, 1)

            def edge_second(i, u):
                pe.wait_ge(hid_ready, tile_of(i, u) + 1)
                nc.tensor.matmul(
                    ps_o[u % 2][:, 0 : J * F], ones_3[:], b2e_3[:], start=True, stop=False, skip_group_check=True
                )
                for pr in range(2):
                    last = nc.tensor.matmul(
                        ps_o[u % 2][:, pr * P : (pr + 1) * P], hid[:, 0, pr * P : (pr + 1) * P], W2e_d[:],
                        start=False, stop=(pr == 1), skip_group_check=True,
                    )
                last.then_inc(mm2_done, 1)

            def sum_by_target(l, hot, bank, ring):
                if l == 0:
                    for j in range(J):
                        last = nc.tensor.matmul(
                            bank[:, 0:F], hot[:, j, :], msg[:, ring, j, :], start=(j == 0), stop=(j == J - 1)
                        )
                    return last
                for pr in range(2):
                    for j in range(J):
                        last = nc.tensor.matmul(
                            bank[:, pr * P : (pr + 1) * P],
                            scaled[:, ring, j, 2 * pr : 2 * pr + 2, :].rearrange("p b f -> p (b f)"),
                            hot[:, j, :], start=(j == 0), stop=(j == J - 1),
                        )
                return last

            def scatter(l, i, u):
                s, ring = tile_of(i, u), u % 2
                pe.reg_load(further, control[0:1, bass.ds(s, 1), 0:1].rearrange("p o v -> p (o v)"))
                pe.wait_ge(msg_ready[l], s + 1)
                sum_by_target(l, onehot[:, ring, :, :], ps_agg[ring], ring).then_inc(scattered[l], 1)
                pe.reg_mov(k_reg, 0)
                with pe.While(lambda: pe.snap(k_reg) < pe.snap(further)):
                    pe.reg_add(k_reg, k_reg, 1)
                    pe.reg_add(x_done, x_done, 1)
                    pe.wait_ge(x_onehot_ready[l], pe.snap(x_done))
                    sum_by_target(l, onehot_x, ps_x, ring).then_inc(x_scattered[l], 1)

            def step0(i, u, last=None):
                scatter(0, i, u)
                if last is None or u + 2 <= last:
                    edge_second(i, u + 2)
                if last is None or u + 3 <= last:
                    edge_first(i, u + 3)
                if last is None or u + 4 <= last:
                    attr_transpose(i, u + 4)

            pe.reg_mov(x_done, 0)
            pe.wait_ge(s_control, 1)
            pe.wait_ge(s_b2e3, 16)
            pe.wait_ge(node_out, PAIRS)
            attr_transpose(0, 0)
            edge_first(0, 0)
            attr_transpose(0, 1)
            for u in range(2):
                edge_second(0, u)
                edge_first(0, u + 1)
                attr_transpose(0, u + 2)
            with pe.Fori(0, BODIES - 1) as i:
                for u in range(BODY):
                    step0(i, u)
            for u in range(BODY + 1):
                step0(BODIES - 1, u, last=BODY)

            pe.reg_mov(x_done, 0)
            with pe.Fori(0, BODIES) as i:
                for u in range(BODY):
                    scatter(1, i, u)
            scatter(1, BODIES, 0)

            pe.wait_ge(all_added, 1)
            for c in range(CHUNKS2):
                if c >= 2:
                    pe.wait_ge(bias_added, c - 1)
                for b in range(CH2):
                    for pr in range(2):
                        last = nc.tensor.matmul(
                            ps_o[c % 2][:, b * F : (b + 1) * F], acc1[:, pr, (c * CH2 + b) * P : (c * CH2 + b + 1) * P], basis[:, pr, :],
                            start=(pr == 0), stop=(pr == 1),
                        )
                last.then_inc(transformed, 1)


_INS = ['x', 'src', 'dst', 'edge_attr_32', 'edge_type_8', 'edge_weight1', 'L0_gnn_W1n', 'L0_gnn_b1n', 'L0_gnn_W2n',
        'L0_gnn_b2n', 'L0_gnn_W1e', 'L0_gnn_b1e', 'L0_gnn_W2e', 'L0_gnn_b2e', 'L0_gnn_res_w', 'L0_gnn_dp_scale',
        'L0_gnn_gamma', 'L0_gnn_beta', 'L1_gnn_weight', 'L1_gnn_w_comp', 'L1_gnn_h_bias']
_OUTS = [((12500, 64), 'float32')]


def kernel(**inputs):
    import numpy as _np
    import concourse.bacc as _bacc
    from concourse import mybir as _mybir
    from concourse.bass_utils import run_bass_kernel_spmd as _run

    nc = _bacc.Bacc("TRN2", target_bir_lowering=False, num_devices=1)
    arrays, args = {}, []
    for name in _INS:
        a = _np.ascontiguousarray(inputs[name])
        arrays[f"in_{name}_dram"] = a
        args.append(nc.dram_tensor(f"in_{name}_dram", a.shape, _mybir.dt.from_np(a.dtype), kind="ExternalInput").ap())
    for i, (shape, dtype) in enumerate(_OUTS):
        dt = _mybir.dt.from_np(_np.dtype(dtype))
        args.append(nc.dram_tensor(f"out_{i}_dram", shape, dt, kind="ExternalOutput").ap())
    bass_gnn_resnorm_d2_kernel(nc, *args)
    r = _run(nc, [arrays], core_ids=[0])
    got = tuple(r.results[0][f"out_{i}_dram"] for i in range(len(_OUTS)))
    return got[0]
```

```python
import concourse.bass as bass
from concourse import mybir
from contextlib import ExitStack


def bass_gnn_resnorm_d2_kernel(
    nc: bass.Bass,
    x: bass.AP,
    src: bass.AP,
    dst: bass.AP,
    edge_attr: bass.AP,
    edge_type: bass.AP,
    edge_weight: bass.AP,
    W1n: bass.AP,
    b1n: bass.AP,
    W2n: bass.AP,
    b2n: bass.AP,
    W1e: bass.AP,
    b1e: bass.AP,
    W2e: bass.AP,
    b2e: bass.AP,
    res_w: bass.AP,
    dp_scale: bass.AP,
    gamma: bass.AP,
    beta: bass.AP,
    rel_basis: bass.AP,
    w_comp: bass.AP,
    h_bias: bass.AP,
    out: bass.AP,
):
    f32 = mybir.dt.float32
    bf16 = mybir.dt.bfloat16
    i32 = mybir.dt.int32
    ALU = mybir.AluOpType
    ACT = mybir.ActivationFunctionType
    AX = mybir.AxisListType

    P = 128
    N, F = x.shape
    E, DE = edge_attr.shape
    R, B = w_comp.shape
    H = W1n.shape[1]
    SLOPE, EPS = 0.1, 1e-5
    assert F == 64 and H == P and DE * 4 == P and B == 4 and 2 * F == P

    NB = -(-N // P)
    LAST_ROWS = N - (NB - 1) * P
    PAIRS = NB // 2
    assert NB == 2 * PAIRS and PAIRS % 2 == 1
    J = 4
    ST = P * J
    FULL = E // ST
    TAIL_P = (E - FULL * ST) // J
    assert TAIL_P * J == E - FULL * ST and 0 < TAIL_P < P
    GROUP = 5
    BODY = 2 * GROUP
    BODIES = FULL // BODY
    assert FULL == BODY * BODIES
    TILES = FULL + 1
    CH = 7
    CHUNKS = NB // CH
    assert CH * CHUNKS == NB and CH * F <= 512

    RC = FULL // P
    R_REST = FULL - RC * P

    node_table = nc.dram_tensor("node_table", (NB * P, F), f32, kind="Internal").ap()
    node_table2 = nc.dram_tensor("node_table2", (NB * P, F), f32, kind="Internal").ap()

    def grouped(a):
        return a[0 : FULL * ST].rearrange("(g s p j) -> g p s j", s=GROUP, p=P, j=J)

    def rest(a):
        return a[FULL * ST : E].rearrange("(p j) -> p j", j=J)

    weight_flat = edge_weight.rearrange("e o -> (e o)")
    attr_groups = edge_attr[0 : FULL * ST, :].rearrange("(g s p j) k -> g p s (j k)", s=GROUP, p=P, j=J)
    attr_rest = edge_attr[FULL * ST : E, :].rearrange("(p j) k -> p (j k)", j=J)

    ctx = ExitStack()
    with ctx:

        def sb(name, shape, dt=f32):
            return ctx.enter_context(nc.sbuf_tensor(name, shape, dt))

        def pb(name, shape, dt=f32):
            return ctx.enter_context(nc.psum_tensor(name, shape, dt))

        def sem(name):
            return ctx.enter_context(nc.semaphore(name))

        x_sb = sb("x_sb", [P, NB, F])
        acc = sb("acc", [P, 2, (NB + 1) * P])
        work = sb("work", [P, NB * F])
        xt_all = work[:, :].rearrange("p (b f) -> p b f", f=F)
        scaled = work[:, 0 : 2 * J * B * F].rearrange("p (r j b f) -> p r j b f", r=2, j=J, b=B)
        work_i = work[:, :].bitcast(i32)
        at_w = 2 * J * B * F
        is_rel = work[:, at_w : at_w + GROUP * J * R].rearrange("p (e r) -> p e r", r=R)
        at_w += GROUP * J * R
        coef_terms = work[:, at_w : at_w + GROUP * J * B * R].rearrange("p (e b r) -> p e b r", b=B, r=R)
        at_w += GROUP * J * B * R
        onehot_x = work[:, at_w : at_w + J * P].rearrange("p (j n) -> p j n", j=J)
        at_w += J * P
        onehot = work[:, at_w : at_w + 2 * J * P].rearrange("p (r j n) -> p r j n", r=2, j=J)
        at_w += 2 * J * P
        centred, squares = (
            work[:, at_w + k * CH * F : at_w + (k + 1) * CH * F].rearrange("p (b f) -> p b f", f=F) for k in range(2)
        )
        assert at_w + 2 * CH * F <= NB * F
        dst_rows = work_i[:, 0 : RC * ST].rearrange("p (c e) -> p c e", c=RC)
        dst_rows_r = work_i[0:R_REST, RC * ST : (RC + 1) * ST]
        dst_rows_t = work_i[0:1, (RC + 1) * ST : (RC + 1) * ST + TAIL_P * J]
        rows = sb("rows", [P, BODY, J, F])
        attr = sb("attr", [P, 2, GROUP, J * DE])
        src_ix = sb("src_ix", [P, 2, GROUP * J], i32)
        dst_ix = sb("dst_ix", [P, 2, GROUP * J], i32)
        GJ = GROUP * J
        attr_flat = attr[:, :, :, :].rearrange("p h s k -> p (h s k)")
        etype = attr_flat[:, 0 : 2 * GJ].bitcast(i32).rearrange("p (h e) -> p h e", h=2)
        enorm = attr_flat[:, 2 * GJ : 4 * GJ].rearrange("p (h e) -> p h e", h=2)
        coef = attr_flat[:, 4 * GJ : (4 + 2 * B) * GJ].rearrange("p (h e b) -> p h e b", h=2, b=B)
        rel = sb("rel", [P, 2, GROUP, J])
        rel_x = sb("rel_x", [P, J])
        x_pair = rows[:, 0, :, :].rearrange("p (k b) f -> p k (b f)", k=2)
        attrT = sb("attrT", [P, P])
        node_xT = [attrT[:], rows[:, 1, 0:2, :].rearrange("p j f -> p (j f)")]
        low = sb("low", [P, 2, 2 * P])
        hid = sb("hid", [P, 2, 2 * P])
        msg = work[:, 0 : 2 * J * F].rearrange("p (r j f) -> p r j f", r=2, j=J)

        ident = sb("ident", [P, P])
        iota_i = work_i[:, NB * F - P : NB * F]
        iota_f = sb("iota_f", [P, P])
        zero_c = sb("zero_c", [P, 1])
        root_ahead = sb("root_ahead", [P, 1])
        b2e_parts = sb("b2e_parts", [1, 3, J, F], bf16)
        W1n_d = sb("W1n_d", [P, 2, H])
        W2n_s = sb("W2n_s", [H, F])
        b1n_c = sb("b1n_c", [H, 1])
        b1n_low = sb("b1n_low", [H, 1])
        b2n_r = sb("b2n_r", [P, F])
        W1e_d = sb("W1e_d", [P, 2, P])
        W2e_d = sb("W2e_d", [P, P])
        b1e_c = sb("b1e_c", [P, 1])
        b1e_low = sb("b1e_low", [P, 1])
        b2e_f = sb("b2e_f", [1, F])
        b2e_res = sb("b2e_res", [1, F])
        b2e_up = sb("b2e_up", [1, F])
        b2e_3 = sb("b2e_3", [3, J * F], bf16)
        ones_3 = sb("ones_3", [3, P], bf16)
        gamma_r = sb("gamma_r", [P, F])
        beta_r = sb("beta_r", [P, F])
        hbias_r = sb("hbias_r", [P, F])
        res_c = sb("res_c", [P, 1])
        dp_c = sb("dp_c", [P, 1])
        scale_c = sb("scale_c", [P, 1])
        basis = sb("basis", [P, 2, F])
        wcomp_r = sb("wcomp_r", [P, R, B])
        RCH = RC + 2
        spans_i = sb("spans_i", [P, RCH, 2], i32)
        spans = sb("spans", [P, RCH, 2])
        base = sb("base", [P, TILES])
        control = sb("control", [1, TILES, 2], i32)
        at_w = 0
        later_least = work[0:1, at_w : at_w + BODIES + 1]
        at_w += BODIES + 1
        chunk_ends = work[0:1, at_w : at_w + CHUNKS - 1]
        at_w += CHUNKS - 1
        is_below = work[0:1, at_w : at_w + BODIES * (CHUNKS - 1)].rearrange("o (i c) -> o i c", c=CHUNKS - 1)
        final = sb("final", [1, BODIES + 1], i32)
        final_f = sb("final_f", [1, BODIES + 1])
        norm_stats = sb("norm_stats", [P, 2, CH])
        mean = norm_stats[:, 0, :]
        var = norm_stats[:, 1, :]

        ps_T = pb("ps_T", [P, P])
        ps_z = pb("ps_z", [P, 512])
        ps_o = [pb(f"ps_o{k}", [P, 512]) for k in range(2)]
        ps_agg = [pb(f"ps_agg{k}", [P, 512]) for k in range(2)]
        ps_x = pb("ps_x", [P, 512])
        ps_fin = pb("ps_fin", [P, 512])
        node_z = [ps_z, ps_x]
        node_psT = [ps_T, ps_agg[0]]

        s_node_const = sem("s_node_const")
        s_edge_const = sem("s_edge_const")
        s_x = sem("s_x")
        s_x_rest = sem("s_x_rest")
        s_rows = sem("s_rows")
        s_pool = sem("s_pool")
        s_zero = sem("s_zero")
        s_b2e = sem("s_b2e")
        s_b2e3 = sem("s_b2e3")
        s_setup = sem("s_setup")
        s_spans = sem("s_spans")
        s_bcast = sem("s_bcast")
        s_control = sem("s_control")
        s_dve = sem("s_dve")
        node_staged = sem("node_staged")
        node_T = sem("node_T")
        node_copied = sem("node_copied")
        node_mm1 = sem("node_mm1")
        node_low = sem("node_low")
        node_hid = sem("node_hid")
        node_mm2 = sem("node_mm2")
        node_out = sem("node_out")
        table_ready = sem("table_ready")
        table2_ready = sem("table2_ready")
        s_out = sem("s_out")

        attr_loaded = [sem(f"attr_loaded{h}") for h in range(2)]
        src_loaded = [[sem(f"src_loaded{l}{h}") for h in range(2)] for l in range(2)]
        dst_loaded = [[sem(f"dst_loaded{l}{h}") for h in range(2)] for l in range(2)]
        type_loaded = [sem(f"type_loaded{h}") for h in range(2)]
        norm_loaded = [sem(f"norm_loaded{h}") for h in range(2)]
        gathered = [[sem(f"gathered{l}_{u}") for u in range(BODY)] for l in range(2)]
        transposed = sem("transposed")
        attr_copied = sem("attr_copied")
        mm1_done = sem("mm1_done")
        low_ready = sem("low_ready")
        hid_ready = sem("hid_ready")
        mm2_done = sem("mm2_done")
        msg_ready = [sem("msg_ready"), sem("scaled_ready")]
        rel_ready = [sem(f"rel_ready{l}") for l in range(2)]
        rel_moved = [sem(f"rel_moved{l}") for l in range(2)]
        s_link = sem("s_link")
        gathers_begun = sem("gathers_begun")
        scattered = [sem(f"scattered{l}") for l in range(2)]
        added = [sem(f"added{l}") for l in range(2)]
        x_onehot_ready = [sem(f"x_onehot_ready{l}") for l in range(2)]
        x_scattered = [sem(f"x_scattered{l}") for l in range(2)]
        x_added = [sem(f"x_added{l}") for l in range(2)]
        chunk_steps = sem("chunk_steps")
        var_ready = sem("var_ready")
        std_ready = sem("std_ready")
        root_tables = sem("root_tables")
        normed = [sem(f"normed{l}") for l in range(2)]
        fin_read = [sem(f"fin_read{l}") for l in range(2)]
        block_copied = [sem(f"block_copied{l}") for l in range(2)]
        block_turned = [sem(f"block_turned{l}") for l in range(2)]
        chunk_zeroed = sem("chunk_zeroed")

        block = ctx.enter_context(nc.Block())

        def tile_of(i, u):
            return i * BODY + u

        def slot_of(u):
            return u % BODY

        def half_of(u):
            return (u % BODY) // GROUP

        def uses(i, u):
            return i + (u // BODY) + 1

        def next_chunk(engine, done, limit, k, work_on):
            engine.reg_load(limit, final[0:1, bass.ds(k, 1)])
            with engine.If(engine.snap(done) < engine.snap(limit)):
                work_on(engine.snap(done, min_val=0, max_val=CHUNKS - 2))
                engine.reg_add(done, done, 1)

        def remaining_chunks(engine, done, limit, work_on):
            engine.reg_load(limit, final[0:1, BODIES : BODIES + 1])
            with engine.While(lambda: engine.snap(done) < engine.snap(limit)):
                work_on(engine.snap(done, min_val=0, max_val=CHUNKS - 2))
                engine.reg_add(done, done, 1)
            work_on(CHUNKS - 1)

        def along_partitions(a):
            return a.rearrange("(p o) -> p o", o=1)

        def to_all(a, n):
            return a.rearrange("(o f) -> o f", o=1).to_broadcast([P, n])

        NODE_CONSTS = (
            (W1n_d[0:F, 0, :], W1n),
            (W1n_d[F:P, 1, :], W1n),
            (b1n_c[:], along_partitions(b1n)),
            (W2n_s[:], W2n),
            (b2n_r[:], to_all(b2n, F)),
            (b2e_f[:], b2e.rearrange("(o f) -> o f", o=1)),
            (res_c[:], to_all(res_w, 1)),
            (dp_c[:], to_all(dp_scale, 1)),
        )
        EDGE_CONSTS = tuple(
            (W1e_d[(2 * pr + h) * DE : (2 * pr + h + 1) * DE, pr, h * F : h * F + F], W1e)
            for pr in range(2) for h in range(2)
        ) + (
            (W2e_d[0:F, 0:F], W2e),
            (W2e_d[F:P, F:P], W2e),
            (b1e_c[0:F, :], along_partitions(b1e)),
            (b1e_c[F:P, :], along_partitions(b1e)),
            (gamma_r[:], to_all(gamma, F)),
            (beta_r[:], to_all(beta, F)),
            (hbias_r[:], to_all(h_bias, F)),
            (basis[:], rel_basis.rearrange("(q b) i o -> (b i) q o", q=2)),
            (wcomp_r[:].rearrange("p r b -> p (r b)"), to_all(w_comp.rearrange("r b -> (r b)"), R * B)),
        )
        ZERO_CUT = (NB + 1) * P // 2
        NORM_AFTER = 2
        CUT = 28
        NODE_STORES = PAIRS // 2 + 1
        ALL_GATHERS = 16 * J

        @block.sync
        def _(sp):
            x_main = x[0 : (NB - 1) * P, :].rearrange("(b p) f -> p b f", p=P)
            sp.dma_start(x_sb[:, 0:CUT, :], x_main[:, 0:CUT, :]).then_inc(s_x, 16)
            sp.wait_ge(s_zero, 4)
            for o, a in NODE_CONSTS:
                sp.dma_start(o, a).then_inc(s_node_const, 16)
            sp.dma_start(
                dst_rows, dst[0 : RC * P * ST].rearrange("(c p e) -> p c e", c=RC, p=P)
            ).then_inc(s_rows, 16)
            sp.dma_start(
                dst_rows_r, dst[RC * P * ST : FULL * ST].rearrange("(p e) -> p e", e=ST)
            ).then_inc(s_rows, 16)
            sp.dma_start(
                dst_rows_t, dst[FULL * ST : E].rearrange("(o e) -> o e", o=1)
            ).then_inc(s_rows, 16)
            sp.dma_start(x_sb[:, CUT : NB - 1, :], x_main[:, CUT:, :]).then_inc(s_x_rest, 16)
            sp.dma_start(x_sb[0:LAST_ROWS, NB - 1, :], x[(NB - 1) * P : N, :]).then_inc(s_x_rest, 16)
            sp.wait_ge(s_b2e, 1)
            sp.dma_start(b2e_3[:], b2e_parts[:].rearrange("o t j f -> o t (j f)")).then_inc(s_b2e3, 16)

            def load_group(l, h, g):
                sp.dma_start(
                    src_ix[:, h, :].rearrange("p (s j) -> p s j", j=J), grouped(src)[g]
                ).then_inc(src_loaded[l][h], 16)
                sp.dma_start(
                    dst_ix[:, h, :].rearrange("p (s j) -> p s j", j=J), grouped(dst)[g]
                ).then_inc(dst_loaded[l][h], 16)
                if l == 0:
                    sp.dma_start(attr[:, h, :, :], attr_groups[g]).then_inc(attr_loaded[h], 16)
                else:
                    sp.dma_start(
                        etype[:, h, :].rearrange("p (s j) -> p s j", j=J), grouped(edge_type)[g]
                    ).then_inc(type_loaded[h], 16)
                    sp.dma_start(
                        enorm[:, h, :].rearrange("p (s j) -> p s j", j=J), grouped(weight_flat)[g]
                    ).then_inc(norm_loaded[h], 16)

            def load_tail(l):
                sp.dma_start(src_ix[0:TAIL_P, 0, 0:J], rest(src)).then_inc(src_loaded[l][0], 16)
                sp.dma_start(dst_ix[0:TAIL_P, 0, 0:J], rest(dst)).then_inc(dst_loaded[l][0], 16)
                if l == 0:
                    sp.dma_start(attr[0:TAIL_P, 0, 0, :], attr_rest).then_inc(attr_loaded[0], 16)
                else:
                    sp.dma_start(etype[0:TAIL_P, 0, 0:J], rest(edge_type)).then_inc(type_loaded[0], 16)
                    sp.dma_start(enorm[0:TAIL_P, 0, 0:J], rest(weight_flat)).then_inc(norm_loaded[0], 16)

            done, limit = (sp.alloc_register(f"sp_{n}") for n in ("done", "limit"))
            table2_chunks = node_table2.rearrange("(c b p) f -> c p b f", c=CHUNKS, p=P)
            out_chunks = out[0 : (CHUNKS - 1) * CH * P, :].rearrange("(c b p) f -> c p b f", b=CH, p=P)

            def store_chunk(l, c):
                sp.wait_ge(normed[l], c + 1)
                if l == 1 and isinstance(c, int):
                    lo, hi = c * CH, NB - 1
                    sp.dma_start(
                        out[lo * P : hi * P, :].rearrange("(b p) f -> p b f", p=P), x_sb[:, lo:hi, :]
                    ).then_inc(s_out, 16)
                    sp.dma_start(out[hi * P : N, :], x_sb[0:LAST_ROWS, hi, :]).then_inc(s_out, 16)
                    return
                sp.dma_start(
                    (table2_chunks, out_chunks)[l][c], x_sb[:, bass.ds(c * CH, CH), :]
                ).then_inc((table2_ready, s_out)[l], 16)

            def layer_loads(l):
                sp.reg_mov(done, 0)
                with sp.Fori(0, BODIES - 1) as i:
                    for h in range(2):
                        sp.wait_ge(msg_ready[l], i * BODY + (h + 1) * GROUP)
                        load_group(l, h, i * 2 + (2 + h))
                    next_chunk(sp, done, limit, i + 1, lambda c: store_chunk(l, c))
                sp.wait_ge(msg_ready[l], (BODIES - 1) * BODY + GROUP)
                load_tail(l)

            for o, a in EDGE_CONSTS:
                sp.dma_start(o, a).then_inc(s_edge_const, 16)
            for h in range(2):
                load_group(0, h, h)
            table_v = node_table[0 : (NB - 2) * P, :].rearrange("(i b p) f -> i p b f", b=4, p=P)
            with sp.Fori(0, PAIRS // 2) as i:
                sp.wait_ge(node_out, i * 2 + 2)
                sp.dma_start(table_v[i], xt_all[:, bass.ds(i * 4, 4), :]).then_inc(table_ready, 16)
            sp.wait_ge(node_out, PAIRS)
            sp.dma_start(
                node_table[(NB - 2) * P :, :].rearrange("(b p) f -> p b f", p=P), xt_all[:, NB - 2 :, :]
            ).then_inc(table_ready, 16)
            layer_loads(0)
            sp.wait_ge(msg_ready[0], TILES)
            for h in range(2):
                load_group(1, h, h)
            remaining_chunks(sp, done, limit, lambda c: store_chunk(0, c))
            layer_loads(1)
            remaining_chunks(sp, done, limit, lambda c: store_chunk(1, c))
            sp.wait_ge(s_out, 16 * (CHUNKS + 1))

        @block.gpsimd
        def _(pool):
            nc.gpsimd.memset(W1n_d[:], 0.0).then_inc(s_zero, 1)
            nc.gpsimd.memset(W1e_d[:], 0.0).then_inc(s_zero, 1)
            nc.gpsimd.memset(W2e_d[:], 0.0).then_inc(s_zero, 1)
            nc.gpsimd.memset(x_sb[:, NB - 1, :], 0.0).then_inc(s_zero, 1)
            nc.gpsimd.memset(ident[:], 0.0).then_inc(s_pool, 1)
            nc.gpsimd.iota(iota_i, pattern=[[1, P]], base=0, channel_multiplier=0).then_inc(s_pool, 1)
            nc.gpsimd.memset(zero_c[:], 0.0).then_inc(s_pool, 1)
            pool.wait_ge(s_pool, 3)
            nc.gpsimd.affine_select(
                out=ident[:], in_=ident[:], compare_op=ALU.not_equal, fill=1.0, base=0,
                pattern=[[-1, P]], channel_multiplier=1,
            ).then_inc(s_pool, 1)
            nc.gpsimd.memset(ones_3[:], 1.0).then_inc(s_pool, 1)
            nc.gpsimd.memset(acc[0:F, 0, 0:ZERO_CUT], 0.0).then_inc(s_pool, 1)

            def stage(q, k):
                nc.gpsimd.tensor_copy(
                    x_pair[:, k, :], x_sb[:, bass.ds(q * 2, 2), :].rearrange("p b f -> p (b f)")
                ).then_inc(node_staged, 1)

            def stage_pairs(first, end):
                with pool.Fori(first // 2, end // 2) as i:
                    for k in range(2):
                        pool.wait_ge(node_T, i * 2 + (k - 1))
                        stage(i * 2 + k, k)

            pool.wait_ge(s_x, 16)
            for q in range(2):
                stage(q, q)
            stage_pairs(2, CUT // 2)
            pool.wait_ge(s_x_rest, 16 * 2)
            stage_pairs(CUT // 2, PAIRS - 1)
            pool.wait_ge(node_T, PAIRS - 2)
            stage(PAIRS - 1, 0)

            def gather(l, i, u, slot_used=None):
                table = (node_table, node_table2)[l]
                if slot_used is not None:
                    pool.wait_ge(msg_ready[l], slot_used)
                if (u % GROUP) == 0:
                    pool.wait_ge(src_loaded[l][half_of(u)], uses(i, u) * 16)
                pool.sem_inc(gathers_begun, 1)
                for j in range(J):
                    col = (u % GROUP) * J + j
                    nc.gpsimd.indirect_dma_start(
                        rows[:, slot_of(u), j, :], None, table,
                        bass.IndirectOffsetOnAxis(ap=src_ix[:, half_of(u), col : col + 1], axis=0),
                    ).then_inc(gathered[l][slot_of(u)], 16)

            for l in range(2):
                ready, count = ((table_ready, 16 * NODE_STORES), (table2_ready, 16 * CHUNKS))[l]
                pool.wait_ge(ready, count)
                for u in range(BODY):
                    gather(l, 0, u)
                with pool.Fori(1, BODIES) as i:
                    for u in range(BODY):
                        gather(l, i, u, i * BODY + (u + 1 - BODY))
                gather(l, BODIES, 0, FULL + 1 - BODY)

        @block.scalar
        def _(act):
            act.wait_ge(s_node_const, 16 * len(NODE_CONSTS))
            nc.scalar.mul(b1n_low[:], b1n_c[:], SLOPE).then_inc(s_setup, 1)
            act.wait_ge(s_setup, 1)

            def node_copy(q, k):
                act.wait_ge(node_T, q + 1)
                nc.scalar.copy(node_xT[k], node_psT[k][:, 0:P]).then_inc(node_copied, 1)

            def node_lower(q, k):
                act.wait_ge(node_mm1, q + 1)
                nc.scalar.activation(
                    low[:, k, :], node_z[k][:, 0 : 2 * P], ACT.Identity, bias=b1n_low[:], scale=SLOPE
                ).then_inc(node_low, 1)

            node_copy(0, 0)
            node_copy(1, 1)
            with act.Fori(0, (PAIRS - 3) // 2) as i:
                for k in range(2):
                    node_lower(i * 2 + k, k)
                    node_copy(i * 2 + (k + 2), k)
            node_lower(PAIRS - 3, 0)
            node_copy(PAIRS - 1, 0)
            node_lower(PAIRS - 2, 1)
            node_lower(PAIRS - 1, 0)
            act.wait_ge(s_edge_const, 16 * len(EDGE_CONSTS))
            nc.scalar.mul(b1e_low[:], b1e_c[:], SLOPE).then_inc(s_setup, 1)
            act.wait_ge(s_setup, 2)

            def edge_copy(i, u):
                act.wait_ge(transposed, tile_of(i, u) + 1)
                nc.scalar.copy(attrT[:], ps_T[:]).then_inc(attr_copied, 1)

            def edge_lower(i, u):
                act.wait_ge(mm1_done, tile_of(i, u) + 1)
                nc.scalar.activation(
                    low[:, 0, :], ps_z[:, 0 : 2 * P], ACT.Identity, bias=b1e_low[:], scale=SLOPE
                ).then_inc(low_ready, 1)

            def step(i, u, last=TILES):
                if last is None or i * BODY + u + 2 < TILES:
                    edge_lower(i, u + 2)
                if last is None or i * BODY + u + 3 < TILES:
                    edge_copy(i, u + 3)

            copied, rooted, limit = (act.alloc_register(f"act_{n}") for n in ("copied", "rooted", "limit"))

            def root(count):
                act.wait_ge(var_ready, count)
                nc.scalar.activation(var, var, ACT.Sqrt).then_inc(std_ready, 1)

            def copy_blocks(l, c, tiles, part):
                act.wait_ge(added[l], tiles + 1)
                for b in range(CH):
                    act.wait_ge(block_turned[l], c * CH + (b + 1))
                    nodes = bass.ds(c * (CH * P) + b * P, P)
                    nc.scalar.copy(*part(b % 2, nodes)).then_inc(block_copied[l], 1)

            def copy0(c, tiles):
                copy_blocks(0, c, tiles, lambda k, nodes: (hid[0:F, 1, k * P : (k + 1) * P], acc[0:F, 0, nodes]))
                act.wait_ge(block_copied[0], c * CH + CH)
                nc.scalar.activation(root_ahead[:], zero_c[:], ACT.Sqrt).then_inc(root_tables, 1)
                n = (CH + isinstance(c, int)) * P
                nc.scalar.copy(
                    acc[:, :, bass.ds(c * (CH * P), n)],
                    zero_c[:].rearrange("p (o n) -> p o n", o=1).to_broadcast([P, 2, n]),
                ).then_inc(chunk_zeroed, 1)

            def roots0(c):
                for norm in range(2):
                    root(c * 2 + (norm + 1))

            def finish1(c, tiles):
                copy_blocks(1, c, tiles, lambda k, nodes: (
                    hid[:, k, :].rearrange("p (q n) -> p q n", q=2), acc[:, :, nodes]))
                root(c + (2 * CHUNKS + 1))

            def finish0(c):
                copy0(c, TILES)
                roots0(c)

            act.reg_mov(copied, 0)
            act.reg_mov(rooted, 0)
            act.wait_ge(s_control, 1)
            edge_copy(0, 0)
            edge_lower(0, 0)
            edge_copy(0, 1)
            edge_lower(0, 1)
            edge_copy(0, 2)
            with act.Fori(0, BODIES - 1) as i:
                for u in range(BODY):
                    step(i, u, None)
                    if u == NORM_AFTER:
                        next_chunk(act, rooted, limit, i, roots0)
                next_chunk(act, copied, limit, i + 1, lambda c: copy0(c, i * BODY + BODY))
            for u in range(BODY + 1):
                step(BODIES - 1, u)
                if u == NORM_AFTER:
                    next_chunk(act, rooted, limit, BODIES - 1, roots0)
            remaining_chunks(act, copied, limit, finish0)
            act.reg_mov(copied, 0)
            with act.Fori(0, BODIES - 1) as i:
                next_chunk(act, copied, limit, i + 1, lambda c: finish1(c, i * BODY + BODY))
            remaining_chunks(act, copied, limit, lambda c: finish1(c, TILES))

        @block.vector
        def _(dve):
            steps = [0]

            def link(ins):
                steps[0] += 1
                ins.then_inc(s_dve, 1)
                dve.wait_ge(s_dve, steps[0])

            dve.wait_ge(s_pool, 3)
            nc.vector.tensor_copy(iota_f[:], iota_i)
            link(nc.vector.memset(spans_i[:], 0))
            nc.vector.memset(acc[0:F, 0, ZERO_CUT:], 0.0)
            dve.wait_ge(s_node_const, 16 * len(NODE_CONSTS))
            link(nc.vector.tensor_tensor(scale_c[:], res_c[:], dp_c[:], ALU.mult))
            rest_of = b2e_f
            for t in range(3):
                part = b2e_parts[:, t, :, :]
                link(nc.vector.tensor_copy(part, rest_of[:].rearrange("o (j f) -> o j f", j=1).to_broadcast([1, J, F])))
                if t < 2:
                    link(nc.vector.tensor_copy(b2e_up[:], b2e_parts[:, t, 0, :]))
                    link(nc.vector.tensor_tensor(b2e_res[:], rest_of[:], b2e_up[:], ALU.subtract))
                    rest_of = b2e_res
            dve.sem_inc(s_b2e, 1)

            dve.wait_ge(s_rows, 16 * 3)
            for v, op in enumerate((ALU.min, ALU.max)):
                nc.vector.tensor_reduce(spans_i[:, 0:RC, v], dst_rows, axis=AX.X, op=op)
                nc.vector.tensor_reduce(spans_i[0:R_REST, RC, v : v + 1], dst_rows_r, axis=AX.X, op=op)
                link(nc.vector.tensor_reduce(spans_i[0:1, RC + 1, v : v + 1], dst_rows_t, axis=AX.X, op=op))
            link(nc.vector.tensor_copy(spans[:], spans_i[:]))
            link(nc.vector.tensor_tensor(spans_i[:, :, 1], spans[:, :, 1], spans[:, :, 0], ALU.subtract))
            link(nc.vector.tensor_scalar(spans_i[:, :, 1], spans_i[:, :, 1], 7, None, ALU.logical_shift_right))
            nc.vector.tensor_copy(spans[:, :, 1], spans_i[:, :, 1]).then_inc(s_spans, 1)
            def node_hidden(q, k):
                dve.wait_ge(node_low, q + 1)
                nc.vector.scalar_tensor_tensor(
                    hid[:, k, :], node_z[k][:, 0 : 2 * P], b1n_c[:], low[:, k, :], ALU.add, ALU.max
                ).then_inc(node_hid, 1)

            def node_store(q, k):
                dve.wait_ge(node_mm2, q + 1)
                nc.vector.tensor_tensor(
                    xt_all[:, bass.ds(q * 2, 2), :],
                    ps_o[k][:, 0 : 2 * F].rearrange("p (b f) -> p b f", b=2),
                    b2n_r[:].rearrange("p (o f) -> p o f", o=1).to_broadcast([P, 2, F]),
                    ALU.add,
                ).then_inc(node_out, 1)

            node_hidden(0, 0)
            with dve.Fori(0, PAIRS // 2) as i:
                for k in range(2):
                    node_hidden(i * 2 + (k + 1), 1 - k)
                    node_store(i * 2 + k, k)
            node_store(PAIRS - 1, 0)

            dve.wait_ge(table_ready, 16 * NODE_STORES)
            dve.wait_ge(s_bcast, 1)
            nc.vector.tensor_copy(control[:, :, 0], ps_agg[1][0:1, 0:TILES])
            nc.vector.tensor_copy(control[:, :, 1], ps_agg[0][0:1, 0:TILES])
            link(nc.vector.tensor_copy(base[:], ps_agg[0][:, 0:TILES]))
            link(nc.vector.tensor_reduce(
                final_f[:, 0:BODIES], base[0:1, 0:FULL].rearrange("o (i u) -> o i u", u=BODY), axis=AX.X, op=ALU.min))
            link(nc.vector.tensor_copy(final_f[:, BODIES:], base[0:1, FULL:]))
            step = 1
            while step < BODIES + 1:
                n = BODIES + 1 - step
                link(nc.vector.tensor_tensor(later_least[:, 0:n], final_f[:, 0:n], final_f[:, step:], ALU.min))
                link(nc.vector.tensor_copy(final_f[:, 0:n], later_least[:, 0:n]))
                step *= 2
            link(nc.vector.tensor_scalar(chunk_ends, iota_f[0:1, 0 : CHUNKS - 1], float(CH * P), float(CH * P), ALU.mult, ALU.add))
            link(nc.vector.tensor_tensor(
                is_below,
                final_f[:, 1:].rearrange("o (i c) -> o i c", c=1).to_broadcast([1, BODIES, CHUNKS - 1]),
                chunk_ends.rearrange("o (i c) -> o i c", i=1).to_broadcast([1, BODIES, CHUNKS - 1]),
                ALU.is_ge))
            link(nc.vector.tensor_reduce(later_least[:, 0:BODIES], is_below, axis=AX.X, op=ALU.add))
            link(nc.vector.memset(later_least[:, BODIES - 1 : BODIES], CHUNKS - 1))
            nc.vector.memset(final[:, 0:1], 0)
            link(nc.vector.tensor_copy(final[:, 1:], later_least[:, 0:BODIES]))
            dve.sem_inc(s_control, 1)
            window, further = (
                [dve.alloc_register(f"dve_{name}{n}") for n in range(2)] for name in ("window", "further")
            )
            k_reg, x_done = (dve.alloc_register(f"dve_{n}") for n in ("k", "x_done"))

            def span_of(i, u):
                dve.reg_load(
                    [further[u % 2], window[u % 2]],
                    control[0:1, bass.ds(tile_of(i, u), 1), :].rearrange("p o v -> p (o v)"),
                )

            def relative(l, i, u):
                h = half_of(u)
                dve.wait_ge(dst_loaded[l][h], uses(i, u) * 16)
                s = tile_of(i, u)
                nc.vector.tensor_tensor(
                    rel[:, h, :, :],
                    dst_ix[:, h, :].rearrange("p (s j) -> p s j", j=J),
                    base[:, bass.ds(s, GROUP)].rearrange("p (s o) -> p s o", o=1).to_broadcast([P, GROUP, J]),
                    ALU.subtract,
                ).then_inc(rel_ready[l], 1)
                dve.wait_ge(rel_ready[l], i * 2 + (u // GROUP) + 1)

            def relative_tail(l):
                dve.wait_ge(dst_loaded[l][0], (BODIES + 1) * 16)
                nc.vector.memset(rel[:, 0, 0, :], -1.0).then_inc(rel_ready[l], 1)
                dve.wait_ge(rel_ready[l], BODIES * 2 + 1)
                nc.vector.tensor_tensor(
                    rel[0:TAIL_P, 0, 0, :],
                    dst_ix[0:TAIL_P, 0, 0:J],
                    base[0:TAIL_P, FULL : FULL + 1].to_broadcast([TAIL_P, J]),
                    ALU.subtract,
                ).then_inc(rel_ready[l], 1)
                dve.wait_ge(rel_ready[l], BODIES * 2 + 2)

            def one_hot(o, r):
                return nc.vector.tensor_tensor(
                    o,
                    iota_f[:].rearrange("p (o n) -> p o n", o=1).to_broadcast([P, J, P]),
                    r.rearrange("p (j o) -> p j o", o=1).to_broadcast([P, J, P]),
                    ALU.is_equal,
                )

            def add_window(l, ring, k, bank):
                nodes = bass.ds(dve.snap(window[ring]) + k * P, P)
                if l == 0:
                    a, sums = acc[0:F, 0, nodes], bank[0:F, 0:P]
                else:
                    a, sums = acc[:, :, nodes], bank[:, 0 : 2 * P].rearrange("p (q n) -> p q n", q=2)
                return nc.vector.tensor_tensor(a, a, sums, ALU.add)

            def add_sums(l, i, u, bank, last=False):
                if last:
                    dve.wait_ge(added[l], FULL + 1)
                dve.wait_ge(scattered[l], tile_of(i, u) + 1)
                add_window(l, u % 2, 0, bank).then_inc(added[l], 1)

            def extras(l, i, u):
                s = tile_of(i, u)
                dve.reg_mov(k_reg, 0)
                with dve.While(lambda: dve.snap(k_reg) < dve.snap(further[u % 2])):
                    r = rel[:, half_of(u), u % GROUP, :]
                    dve.wait_ge(added[l], s + 2)
                    dve.reg_add(x_done, x_done, 1)
                    nc.vector.tensor_scalar(r, r, float(P), None, ALU.subtract).then_inc(rel_moved[l], 1)
                    dve.wait_ge(rel_moved[l], dve.snap(x_done))
                    one_hot(onehot_x, r).then_inc(x_onehot_ready[l], 1)
                    dve.wait_ge(x_scattered[l], dve.snap(x_done))
                    add_window(l, u % 2, dve.snap(k_reg) + 1, ps_x).then_inc(x_added[l], 1)
                    dve.wait_ge(x_added[l], dve.snap(x_done))
                    dve.reg_add(k_reg, k_reg, 1)

            def main_one_hot(l, i, u):
                if u > 0 or not (isinstance(i, int) and i == 0):
                    dve.wait_ge(added[l], tile_of(i, u))
                one_hot(onehot[:, u % 2, :, :], rel[:, half_of(u), u % GROUP, :])

            def edge_hidden(i, u):
                dve.wait_ge(low_ready, tile_of(i, u) + 1)
                nc.vector.scalar_tensor_tensor(
                    hid[:, 0, :], ps_z[:, 0 : 2 * P], b1e_c[:], low[:, 0, :], ALU.add, ALU.max
                ).then_inc(hid_ready, 1)

            def message(i, u):
                dve.wait_ge(gathered[0][slot_of(u)], uses(i, u) * ALL_GATHERS)
                dve.wait_ge(mm2_done, tile_of(i, u) + 1)
                nc.vector.tensor_tensor(
                    msg[:, u % 2, :, :].rearrange("p j f -> p (j f)"),
                    ps_o[u % 2][:, 0 : J * F],
                    rows[:, slot_of(u), :, :].rearrange("p j f -> p (j f)"),
                    ALU.mult,
                ).then_inc(msg_ready[0], 1)

            def prepare0(i, u, tail=False):
                span_of(i, u)
                if tail:
                    relative_tail(0)
                elif u % GROUP == 0:
                    relative(0, i, u)
                main_one_hot(0, i, u)
                message(i, u)

            def step0(i, u, last=None):
                if last is None or u + 1 <= last:
                    prepare0(i, u + 1, tail=(last is not None and u + 1 == last))
                if last is None or u + 2 <= last:
                    edge_hidden(i, u + 2)
                add_sums(0, i, u, ps_agg[u % 2], last is not None and u == last)
                extras(0, i, u)

            dve.wait_ge(s_pool, 6)
            dve.wait_ge(s_edge_const, 16 * len(EDGE_CONSTS))
            for l in range(2):
                dve.sem_inc(added[l], 1)
                dve.sem_inc(fin_read[l], 1)
            done, limit = (dve.alloc_register(f"dve_{n}") for n in ("done", "limit"))
            STEPS0, STEPS1 = 18, 9

            def over_features(ap):
                return ap.rearrange("p (b o) -> p b o", o=1).to_broadcast([P, CH, F])

            def over_blocks(ap):
                return ap.rearrange("p (o f) -> p o f", o=1).to_broadcast([P, CH, F])

            def in_chunk(c, l):
                taken = [0]

                def link_c(ins):
                    taken[0] += 1
                    ins.then_inc(chunk_steps, 1)
                    first = c * STEPS0 if l == 0 else c * STEPS1 + CHUNKS * STEPS0
                    dve.wait_ge(chunk_steps, first + taken[0])

                return link_c, taken

            def layer_norm(link_c, count, target):
                link_c(nc.vector.tensor_reduce(mean, centred, axis=AX.X, op=ALU.add))
                link_c(nc.vector.tensor_scalar(mean, mean, 1.0 / F, None, ALU.mult))
                link_c(nc.vector.tensor_tensor(centred, centred, over_features(mean), ALU.subtract))
                link_c(nc.vector.tensor_tensor(squares, centred, centred, ALU.mult))
                link_c(nc.vector.tensor_reduce(var, squares, axis=AX.X, op=ALU.add))
                nc.vector.tensor_scalar(var, var, 1.0 / F, EPS, ALU.mult, ALU.add).then_inc(var_ready, 1)
                dve.wait_ge(std_ready, count)
                link_c(nc.vector.reciprocal(var, var))
                return nc.vector.tensor_tensor(target, centred, over_features(var), ALU.mult)

            def finish0(c):
                link_c, taken = in_chunk(c, 0)
                x_c = x_sb[:, bass.ds(c * CH, CH), :]
                dve.wait_ge(block_turned[0], c * CH + (CH + 2))
                link_c(nc.vector.scalar_tensor_tensor(
                    centred, ps_fin[:, 0 : CH * F].rearrange("p (b f) -> p b f", f=F), scale_c[:], x_c,
                    ALU.mult, ALU.add))
                dve.sem_inc(fin_read[0], 1)
                link_c(layer_norm(link_c, c * 2 + 1, centred))
                link_c(nc.vector.tensor_tensor(centred, centred, over_blocks(gamma_r[:]), ALU.mult))
                link_c(nc.vector.tensor_tensor(centred, centred, over_blocks(beta_r[:]), ALU.add))
                link_c(nc.vector.tensor_tensor(centred, centred, x_c, ALU.add))
                link_c(layer_norm(link_c, c * 2 + 2, x_c))
                assert taken[0] == STEPS0, taken
                dve.sem_inc(normed[0], 1)

            def finish1(c):
                link_c, taken = in_chunk(c, 1)
                dve.wait_ge(block_turned[1], c * CH + (CH + 2))
                link_c(nc.vector.tensor_tensor(
                    centred, ps_fin[:, 0 : CH * F].rearrange("p (b f) -> p b f", f=F), over_blocks(hbias_r[:]), ALU.add))
                dve.sem_inc(fin_read[1], 1)
                x_c = x_sb[:, bass.ds(c * CH, CH), :]
                link_c(nc.vector.scalar_tensor_tensor(centred, centred, 0.0, x_c, ALU.max, ALU.add))
                link_c(layer_norm(link_c, c + (2 * CHUNKS + 1), x_c))
                dve.sem_inc(normed[1], 1)
                assert taken[0] == STEPS1, taken

            dve.reg_mov(done, 0)
            dve.reg_mov(x_done, 0)
            edge_hidden(0, 0)
            edge_hidden(0, 1)
            prepare0(0, 0)
            with dve.Fori(0, BODIES - 1) as i:
                for u in range(BODY):
                    step0(i, u)
                    if u == NORM_AFTER:
                        next_chunk(dve, done, limit, i, finish0)
            for u in range(BODY + 1):
                step0(BODIES - 1, u, last=BODY)
                if u == NORM_AFTER:
                    next_chunk(dve, done, limit, BODIES - 1, finish0)
            remaining_chunks(dve, done, limit, finish0)

            def coefficients(i, u, rows_p=P, cols=GROUP * J):
                h = half_of(u)
                dve.wait_ge(type_loaded[h], uses(i, u) * 16)
                link_l(nc.vector.tensor_tensor(
                    is_rel,
                    etype[:, h, :].rearrange("p (e o) -> p e o", o=1).to_broadcast([P, GROUP * J, R]),
                    iota_f[:, 0:R].rearrange("p (o r) -> p o r", o=1).to_broadcast([P, GROUP * J, R]),
                    ALU.is_equal))
                dve.wait_ge(norm_loaded[h], uses(i, u) * 16)
                link_l(nc.vector.tensor_tensor(
                    is_rel, is_rel,
                    enorm[:, h, :].rearrange("p (e o) -> p e o", o=1).to_broadcast([P, GROUP * J, R]),
                    ALU.mult))
                link_l(nc.vector.tensor_tensor(
                    coef_terms,
                    is_rel.rearrange("p e (o r) -> p e o r", o=1).to_broadcast([P, GROUP * J, B, R]),
                    wcomp_r[:].rearrange("p r b -> p b r").rearrange("p (o b) r -> p o b r", o=1).to_broadcast([P, GROUP * J, B, R]),
                    ALU.mult))
                link_l(nc.vector.tensor_reduce(coef[:, h, :, :], coef_terms, axis=AX.X, op=ALU.add))

            l_steps = dve.alloc_register("dve_link")
            dve.reg_mov(l_steps, 0)

            def link_l(ins):
                ins.then_inc(s_link, 1)
                dve.reg_add(l_steps, l_steps, 1)
                dve.wait_ge(s_link, dve.snap(l_steps))

            def scale_rows(i, u, ring):
                dve.wait_ge(gathered[1][slot_of(u)], uses(i, u) * ALL_GATHERS)
                h, at = half_of(u), (u % GROUP) * J
                nc.vector.tensor_tensor(
                    scaled[:, ring, :, :, :],
                    rows[:, slot_of(u), :, :].rearrange("p j (o f) -> p j o f", o=1).to_broadcast([P, J, B, F]),
                    coef[:, h, at : at + J, :].rearrange("p j (b o) -> p j b o", o=1).to_broadcast([P, J, B, F]),
                    ALU.mult,
                ).then_inc(msg_ready[1], 1)

            def prepare1(i, u, tail=False):
                if tail:
                    relative_tail(1)
                    coefficients(i, u)
                elif u % GROUP == 0:
                    relative(1, i, u)
                    coefficients(i, u)
                main_one_hot(1, i, u)
                scale_rows(i, u, u % 2)

            def add_supertile1(i, u, last=False):
                add_sums(1, i, u, ps_agg[u % 2], last)
                extras(1, i, u)

            dve.wait_ge(chunk_zeroed, CHUNKS)
            dve.reg_mov(done, 0)
            dve.reg_mov(x_done, 0)
            prepare1(0, 0)
            with dve.Fori(0, BODIES - 1) as i:
                for u in range(BODY):
                    span_of(i, u)
                    prepare1(i, u + 1)
                    add_supertile1(i, u)
                    if u == NORM_AFTER:
                        next_chunk(dve, done, limit, i, finish1)
            for u in range(BODY + 1):
                span_of(BODIES - 1, u)
                if u < BODY:
                    prepare1(BODIES - 1, u + 1, tail=(u + 1 == BODY))
                add_supertile1(BODIES - 1, u, u == BODY)
                if u == NORM_AFTER:
                    next_chunk(dve, done, limit, BODIES - 1, finish1)
            remaining_chunks(dve, done, limit, finish1)

        @block.tensor
        def _(pe):
            pe.wait_ge(s_pool, 5)
            def node_transpose(q, k):
                pe.wait_ge(node_staged, q + 1)
                nc.tensor.transpose(node_psT[k][:, 0:P], x_pair[:, k, :], ident[:]).then_inc(node_T, 1)

            def node_first(q, k):
                pe.wait_ge(node_copied, q + 1)
                for b in range(2):
                    last = nc.tensor.matmul(
                        node_z[k][:, b * P : (b + 1) * P], W1n_d[:, b, :], node_xT[k], start=True, stop=True
                    )
                last.then_inc(node_mm1, 1)

            def node_second(q, k):
                pe.wait_ge(node_hid, q + 1)
                for b in range(2):
                    last = nc.tensor.matmul(
                        ps_o[k][:, b * F : (b + 1) * F], hid[:, k, b * P : (b + 1) * P], W2n_s[:],
                        start=True, stop=True,
                    )
                last.then_inc(node_mm2, 1)

            pe.wait_ge(s_node_const, 16 * len(NODE_CONSTS))
            node_transpose(0, 0)
            node_transpose(1, 1)
            node_first(0, 0)
            node_transpose(2, 0)
            with pe.Fori(0, (PAIRS - 3) // 2) as i:
                for k in range(2):
                    node_first(i * 2 + (k + 1), 1 - k)
                    node_transpose(i * 2 + (k + 3), 1 - k)
                    node_second(i * 2 + k, k)
            node_first(PAIRS - 2, 1)
            node_second(PAIRS - 3, 0)
            node_first(PAIRS - 1, 0)
            node_second(PAIRS - 2, 1)
            node_second(PAIRS - 1, 0)
            pe.wait_ge(s_spans, 1)
            for v in range(2):
                for c in range(RCH):
                    rows_c = (P, R_REST, 1)[max(0, c - RC + 1)]
                    at = FULL if c == RCH - 1 else c * P
                    last = nc.tensor.matmul(
                        ps_agg[v][:, at : at + rows_c],
                        spans[0:rows_c, c, v : v + 1].to_broadcast([rows_c, P]),
                        ident[0:rows_c, 0:rows_c], start=True, stop=True,
                    )
            last.then_inc(s_bcast, 1)

            further, k_reg, x_done = (pe.alloc_register(f"pe_{n}") for n in ("further", "k", "x_done"))

            def attr_transpose(i, u):
                if u % GROUP == 0:
                    pe.wait_ge(attr_loaded[half_of(u)], uses(i, u) * 16)
                nc.tensor.transpose(ps_T[:], attr[:, half_of(u), u % GROUP, :], ident[:]).then_inc(
                    transposed, 1
                )

            def edge_first(i, u):
                pe.wait_ge(attr_copied, tile_of(i, u) + 1)
                for pr in range(2):
                    last = nc.tensor.matmul(
                        ps_z[:, pr * P : (pr + 1) * P], W1e_d[:, pr, :], attrT[:], start=True, stop=True
                    )
                last.then_inc(mm1_done, 1)

            def edge_second(i, u):
                pe.wait_ge(hid_ready, tile_of(i, u) + 1)
                nc.tensor.matmul(
                    ps_o[u % 2][:, 0 : J * F], ones_3[:], b2e_3[:], start=True, stop=False, skip_group_check=True
                )
                for pr in range(2):
                    last = nc.tensor.matmul(
                        ps_o[u % 2][:, pr * P : (pr + 1) * P], hid[:, 0, pr * P : (pr + 1) * P], W2e_d[:],
                        start=False, stop=(pr == 1), skip_group_check=True,
                    )
                last.then_inc(mm2_done, 1)

            def sum_by_target(l, hot, bank, ring):
                if l == 0:
                    for j in range(J):
                        last = nc.tensor.matmul(
                            bank[0:F, 0:P], msg[:, ring, j, :], hot[:, j, :], start=(j == 0), stop=(j == J - 1)
                        )
                    return last
                for pr in range(2):
                    for j in range(J):
                        last = nc.tensor.matmul(
                            bank[:, pr * P : (pr + 1) * P],
                            scaled[:, ring, j, 2 * pr : 2 * pr + 2, :].rearrange("p b f -> p (b f)"),
                            hot[:, j, :], start=(j == 0), stop=(j == J - 1),
                        )
                return last

            def scatter(l, i, u):
                s, ring = tile_of(i, u), u % 2
                pe.reg_load(further, control[0:1, bass.ds(s, 1), 0:1].rearrange("p o v -> p (o v)"))
                pe.wait_ge(msg_ready[l], s + 1)
                sum_by_target(l, onehot[:, ring, :, :], ps_agg[ring], ring).then_inc(scattered[l], 1)
                pe.reg_mov(k_reg, 0)
                with pe.While(lambda: pe.snap(k_reg) < pe.snap(further)):
                    pe.reg_add(k_reg, k_reg, 1)
                    pe.reg_add(x_done, x_done, 1)
                    pe.wait_ge(x_onehot_ready[l], pe.snap(x_done))
                    sum_by_target(l, onehot_x, ps_x, ring).then_inc(x_scattered[l], 1)

            def step0(i, u, last=None):
                scatter(0, i, u)
                if last is None or u + 2 <= last:
                    edge_second(i, u + 2)
                if last is None or u + 3 <= last:
                    edge_first(i, u + 3)
                if last is None or u + 4 <= last:
                    attr_transpose(i, u + 4)

            done, limit = (pe.alloc_register(f"pe_{n}") for n in ("done", "limit"))

            def finish0(c):
                pe.wait_ge(fin_read[0], c + 1)
                for b in range(CH):
                    pe.wait_ge(block_copied[0], c * CH + (b + 1))
                    k = b % 2
                    nc.tensor.matmul(
                        ps_fin[:, b * F : (b + 1) * F], hid[0:F, 1, k * P : (k + 1) * P], ident[0:F, 0:F],
                        start=True, stop=True,
                    ).then_inc(block_turned[0], 1)

            for l in range(2):
                pe.sem_inc(block_turned[l], 2)
            pe.reg_mov(done, 0)
            pe.reg_mov(x_done, 0)
            pe.wait_ge(s_control, 1)
            pe.wait_ge(s_b2e3, 16)
            pe.wait_ge(s_edge_const, 16 * len(EDGE_CONSTS))
            pe.wait_ge(node_out, PAIRS)
            attr_transpose(0, 0)
            edge_first(0, 0)
            attr_transpose(0, 1)
            for u in range(2):
                edge_second(0, u)
                edge_first(0, u + 1)
                attr_transpose(0, u + 2)
            with pe.Fori(0, BODIES - 1) as i:
                for u in range(BODY):
                    step0(i, u)
                next_chunk(pe, done, limit, i + 1, finish0)
            for u in range(BODY + 1):
                step0(BODIES - 1, u, last=BODY)
            remaining_chunks(pe, done, limit, finish0)

            def finish1(c):
                pe.wait_ge(fin_read[1], c + 1)
                for b in range(CH):
                    pe.wait_ge(block_copied[1], c * CH + (b + 1))
                    for pr in range(2):
                        last = nc.tensor.matmul(
                            ps_fin[:, b * F : (b + 1) * F], hid[:, b % 2, pr * P : (pr + 1) * P], basis[:, pr, :],
                            start=(pr == 0), stop=(pr == 1),
                        )
                    last.then_inc(block_turned[1], 1)

            pe.reg_mov(done, 0)
            pe.reg_mov(x_done, 0)
            with pe.Fori(0, BODIES - 1) as i:
                for u in range(BODY):
                    scatter(1, i, u)
                next_chunk(pe, done, limit, i + 1, finish1)
            for u in range(BODY + 1):
                scatter(1, BODIES - 1, u)
            remaining_chunks(pe, done, limit, finish1)


_INS = ['x', 'src', 'dst', 'edge_attr_32', 'edge_type_8', 'edge_weight1', 'L0_gnn_W1n', 'L0_gnn_b1n', 'L0_gnn_W2n',
        'L0_gnn_b2n', 'L0_gnn_W1e', 'L0_gnn_b1e', 'L0_gnn_W2e', 'L0_gnn_b2e', 'L0_gnn_res_w', 'L0_gnn_dp_scale',
        'L0_gnn_gamma', 'L0_gnn_beta', 'L1_gnn_weight', 'L1_gnn_w_comp', 'L1_gnn_h_bias']
_OUTS = [((12500, 64), 'float32')]


def kernel(**inputs):
    import numpy as _np
    import concourse.bacc as _bacc
    from concourse import mybir as _mybir
    from concourse.bass_utils import run_bass_kernel_spmd as _run

    nc = _bacc.Bacc("TRN2", target_bir_lowering=False, num_devices=1)
    arrays, args = {}, []
    for name in _INS:
        a = _np.ascontiguousarray(inputs[name])
        arrays[f"in_{name}_dram"] = a
        args.append(nc.dram_tensor(f"in_{name}_dram", a.shape, _mybir.dt.from_np(a.dtype), kind="ExternalInput").ap())
    for i, (shape, dtype) in enumerate(_OUTS):
        dt = _mybir.dt.from_np(_np.dtype(dtype))
        args.append(nc.dram_tensor(f"out_{i}_dram", shape, dt, kind="ExternalOutput").ap())
    bass_gnn_resnorm_d2_kernel(nc, *args)
    r = _run(nc, [arrays], core_ids=[0])
    got = tuple(r.results[0][f"out_{i}_dram"] for i in range(len(_OUTS)))
    return got[0]
```
